# Optimizing a Trainium2 kernel written in Bass

```python
import numpy as np
import jax
import jax.numpy as jnp

def _softmax(x, axis=-1):
    return jax.nn.softmax(x, axis=axis)

def _gelu(x):
    return jax.nn.gelu(x, approximate=True)

def _silu(x):
    return jax.nn.silu(x)

def _sigmoid(x):
    return jax.nn.sigmoid(x)

def _layernorm(x, axis=-1, eps=1e-05):
    m = jnp.mean(x, axis=axis, keepdims=True)
    v = jnp.var(x, axis=axis, keepdims=True)
    return (x - m) / jnp.sqrt(v + eps)

def _scatter_add(tgt, idx, src, axis=0):
    return tgt.at[idx].add(src)

def _segment_sum(src, seg, n):
    return jax.ops.segment_sum(src, seg, n)
kernel_name = 'mk_gnn_resnorm_d4_gnn_r32_b8b70f'

def setup_inputs(seed: int=0):
    np.random.seed(seed)
    _w = jnp.asarray

    def _rec_inputs():
        import jax
        import jax.numpy as jnp
        _gk = jax.random.key(seed)
        x = -0.000202 + 1 * jax.random.normal(jax.random.fold_in(_gk, 1), (3125, 128), jnp.float32)
        src = jax.random.randint(jax.random.fold_in(_gk, 2), (100000,), 0, 3125, jnp.int32)
        dst = jnp.minimum((3125 * jax.random.uniform(jax.random.fold_in(_gk, 3), (100000,)) ** 2.0).astype(jnp.int32), 99999)
        _o = jnp.argsort(dst, stable=True)
        src = src[_o]
        dst = dst[_o]
        edge_weight = jax.random.uniform(jax.random.fold_in(_gk, 12), (100000,), jnp.float32, 0.0, 0.999999)
        return (x, src, dst, edge_weight)
    x, src, dst, edge_weight = _rec_inputs()

    def _L0_gnn_setup():
        import jax, jax.numpy as jnp
        import numpy as np
        N = 50000
        E = 18750
        F_IN = 128
        F_HID = 512

        def gcn_conv(x, edge_index, W, b):
            n = x.shape[0]
            loop = jnp.arange(n)
            src = jnp.concatenate([edge_index[0], loop])
            dst = jnp.concatenate([edge_index[1], loop])
            xw = x @ W.T
            deg = jax.ops.segment_sum(jnp.ones_like(dst, dtype=x.dtype), dst, num_segments=n)
            dinv = jnp.where(deg > 0, jax.lax.rsqrt(deg), 0.0)
            norm = dinv[src] * dinv[dst]
            msg = xw[src] * norm[:, None]
            out = jax.ops.segment_sum(msg, dst, num_segments=n)
            return out + b
        key = jax.random.key(seed)
        k = jax.random.split(key, 7)
        x = jax.random.normal(k[0], (N, F_IN), dtype=jnp.float32)
        edge_index = jax.random.randint(k[1], (2, E), 0, N, dtype=jnp.int64)
        s1 = float(np.sqrt(1.0 / F_IN))
        s2 = float(np.sqrt(1.0 / F_HID))
        W1 = jax.random.uniform(k[2], (F_HID, F_IN), jnp.float32, -s1, s1)
        b1 = jnp.zeros((F_HID,), jnp.float32)
        W2 = jax.random.uniform(k[3], (F_IN, F_HID), jnp.float32, -s2, s2)
        b2 = jnp.zeros((F_IN,), jnp.float32)
        return {'x': x, 'edge_index': edge_index, 'W1': W1, 'b1': b1, 'W2': W2, 'b2': b2}
    _L0_gnn_all = _L0_gnn_setup()
    _L0_gnn_in = {k: v for k, v in _L0_gnn_all.items() if k in ('W1', 'b1', 'W2', 'b2')}
    del _L0_gnn_all

    def _L1_gnn_setup():
        import jax, jax.numpy as jnp
        import numpy as np
        N = 50000
        E = 25000
        IN = 128
        H = 4
        C = 32
        OUT = H * C
        NEG_SLOPE = 0.2
        LN_EPS = 1e-05
        key = jax.random.key(seed)
        ks = jax.random.split(key, 10)
        s = 0.1
        return {'x': jax.random.normal(ks[0], (N, IN), jnp.float32), 'edge_index': jax.random.randint(ks[1], (2, E), 0, N, jnp.int32), 'W': jax.random.normal(ks[2], (IN, H * C), jnp.float32) * s, 'att_src': jax.random.normal(ks[3], (H, C), jnp.float32) * s, 'att_dst': jax.random.normal(ks[4], (H, C), jnp.float32) * s, 'bias': jax.random.normal(ks[5], (H * C,), jnp.float32) * s, 'ln_w': jnp.ones((OUT,), jnp.float32), 'ln_b': jnp.zeros((OUT,), jnp.float32), 'prelu_w': jnp.full((1,), 0.25, jnp.float32)}
    _L1_gnn_all = _L1_gnn_setup()
    _L1_gnn_in = {k: v for k, v in _L1_gnn_all.items() if k in ('W', 'att_src', 'att_dst', 'bias', 'ln_w', 'ln_b', 'prelu_w')}
    del _L1_gnn_all

    def _L2_gnn_setup():
        import jax, jax.numpy as jnp
        import numpy as np
        N_NODES = 50000
        N_EDGES = 50000
        IN_DIM = 128
        N_HEADS = 8
        OUT_DIM = 128
        HEAD_DIM = OUT_DIM // N_HEADS
        key = jax.random.key(seed)
        k1, k2, k3, k4, k5, k6, k7 = jax.random.split(key, 7)
        og_x = jax.random.normal(k1, (N_NODES, IN_DIM), dtype=jnp.float32)
        edge_index = jax.random.randint(k2, (2, N_EDGES), 0, N_NODES, dtype=jnp.int32)
        edge_weight = jax.random.uniform(k3, (N_EDGES,), dtype=jnp.float32)
        s_lin = float(np.sqrt(6.0 / (IN_DIM + OUT_DIM)))
        W = jax.random.uniform(k4, (IN_DIM, OUT_DIM), jnp.float32, -s_lin, s_lin)
        s_att = float(np.sqrt(6.0 / (N_HEADS * HEAD_DIM + 1)))
        att_l = jax.random.uniform(k5, (1, N_HEADS, HEAD_DIM), jnp.float32, -s_att, s_att)
        att_r = jax.random.uniform(k6, (1, N_HEADS, HEAD_DIM), jnp.float32, -s_att, s_att)
        W_res = jax.random.uniform(k7, (IN_DIM, OUT_DIM), jnp.float32, -s_lin, s_lin)
        return {'og_x': og_x, 'edge_index': edge_index, 'edge_weight': edge_weight, 'W': W, 'att_l': att_l, 'att_r': att_r, 'W_res': W_res}
    _L2_gnn_all = _L2_gnn_setup()
    _L2_gnn_in = {k: v for k, v in _L2_gnn_all.items() if k in ('W', 'att_l', 'att_r', 'W_res')}
    del _L2_gnn_all

    def _L3_gnn_setup():
        import jax, jax.numpy as jnp
        import numpy as np
        N = 50000
        E = 25000
        DIN = 128
        H = 4
        C = 32
        EPS = 1e-05
        NEG_SLOPE = 0.2

        def layer_norm(x, g, b):
            m = jnp.mean(x, axis=-1, keepdims=True)
            v = jnp.mean((x - m) ** 2, axis=-1, keepdims=True)
            return (x - m) * jax.lax.rsqrt(v + EPS) * g + b

        def gat_conv(h, src, dst, W, att_src, att_dst, gat_b, n):
            xh = (h @ W).reshape(n, H, C)
            a_src = jnp.einsum('nhc,hc->nh', xh, att_src)
            a_dst = jnp.einsum('nhc,hc->nh', xh, att_dst)
            alpha = jax.nn.leaky_relu(a_src[src] + a_dst[dst], NEG_SLOPE)
            amax = jax.ops.segment_max(alpha, dst, num_segments=n)
            alpha = jnp.exp(alpha - amax[dst])
            denom = jax.ops.segment_sum(alpha, dst, num_segments=n)
            alpha = alpha / denom[dst]
            msg = xh[src] * alpha[:, :, None]
            out = jax.ops.segment_sum(msg, dst, num_segments=n)
            return out.reshape(n, H * C) + gat_b
        key = jax.random.key(seed)
        ks = jax.random.split(key, 14)
        s = 1.0 / np.sqrt(DIN)
        return {'x': jax.random.normal(ks[0], (N, DIN), dtype=jnp.float32), 'edge_index': jax.random.randint(ks[1], (2, E), 0, N, dtype=jnp.int64), 'ln1_g': jnp.ones((DIN,), jnp.float32), 'ln1_b': jnp.zeros((DIN,), jnp.float32), 'W': jax.random.normal(ks[2], (DIN, H * C), jnp.float32) * s, 'att_src': jax.random.normal(ks[3], (H, C), jnp.float32) * (1.0 / np.sqrt(C)), 'att_dst': jax.random.normal(ks[4], (H, C), jnp.float32) * (1.0 / np.sqrt(C)), 'gat_b': jnp.zeros((H * C,), jnp.float32), 'ln2_g': jnp.ones((H * C,), jnp.float32), 'ln2_b': jnp.zeros((H * C,), jnp.float32), 'w1': jax.random.normal(ks[5], (H * C, 2 * H * C), jnp.float32) * (1.0 / np.sqrt(H * C)), 'b1': jnp.zeros((2 * H * C,), jnp.float32), 'w2': jax.random.normal(ks[6], (2 * H * C, H * C), jnp.float32) * (1.0 / np.sqrt(2 * H * C)), 'b2': jnp.zeros((H * C,), jnp.float32)}
    _L3_gnn_all = _L3_gnn_setup()
    _L3_gnn_in = {k: v for k, v in _L3_gnn_all.items() if k in ('ln1_g', 'ln1_b', 'W', 'att_src', 'att_dst', 'gat_b', 'ln2_g', 'ln2_b', 'w1', 'b1', 'w2', 'b2')}
    del _L3_gnn_all
    return {'x': x, 'src': src, 'dst': dst, 'edge_weight': edge_weight, 'L0_gnn_W1': _L0_gnn_in['W1'], 'L0_gnn_b1': _L0_gnn_in['b1'], 'L0_gnn_W2': _L0_gnn_in['W2'], 'L0_gnn_b2': _L0_gnn_in['b2'], 'L1_gnn_W': _L1_gnn_in['W'], 'L1_gnn_att_src': _L1_gnn_in['att_src'], 'L1_gnn_att_dst': _L1_gnn_in['att_dst'], 'L1_gnn_bias': _L1_gnn_in['bias'], 'L1_gnn_ln_w': _L1_gnn_in['ln_w'], 'L1_gnn_ln_b': _L1_gnn_in['ln_b'], 'L1_gnn_prelu_w': _L1_gnn_in['prelu_w'], 'L2_gnn_W': _L2_gnn_in['W'], 'L2_gnn_att_l': _L2_gnn_in['att_l'], 'L2_gnn_att_r': _L2_gnn_in['att_r'], 'L2_gnn_W_res': _L2_gnn_in['W_res'], 'L3_gnn_ln1_g': _L3_gnn_in['ln1_g'], 'L3_gnn_ln1_b': _L3_gnn_in['ln1_b'], 'L3_gnn_W': _L3_gnn_in['W'], 'L3_gnn_att_src': _L3_gnn_in['att_src'], 'L3_gnn_att_dst': _L3_gnn_in['att_dst'], 'L3_gnn_gat_b': _L3_gnn_in['gat_b'], 'L3_gnn_ln2_g': _L3_gnn_in['ln2_g'], 'L3_gnn_ln2_b': _L3_gnn_in['ln2_b'], 'L3_gnn_w1': _L3_gnn_in['w1'], 'L3_gnn_b1': _L3_gnn_in['b1'], 'L3_gnn_w2': _L3_gnn_in['w2'], 'L3_gnn_b2': _L3_gnn_in['b2']}

def reference(x, src, dst, edge_weight, L0_gnn_W1, L0_gnn_b1, L0_gnn_W2, L0_gnn_b2, L1_gnn_W, L1_gnn_att_src, L1_gnn_att_dst, L1_gnn_bias, L1_gnn_ln_w, L1_gnn_ln_b, L1_gnn_prelu_w, L2_gnn_W, L2_gnn_att_l, L2_gnn_att_r, L2_gnn_W_res, L3_gnn_ln1_g, L3_gnn_ln1_b, L3_gnn_W, L3_gnn_att_src, L3_gnn_att_dst, L3_gnn_gat_b, L3_gnn_ln2_g, L3_gnn_ln2_b, L3_gnn_w1, L3_gnn_b1, L3_gnn_w2, L3_gnn_b2):
    import jax
    import jax.numpy as jnp

    def _L0_gnn_ref(x, edge_index, W1, b1, W2, b2):
        import jax, jax.numpy as jnp
        import numpy as np
        N = 50000
        E = 18750
        F_IN = 128
        F_HID = 512

        def gcn_conv(x, edge_index, W, b):
            n = x.shape[0]
            loop = jnp.arange(n)
            src = jnp.concatenate([edge_index[0], loop])
            dst = jnp.concatenate([edge_index[1], loop])
            xw = x @ W.T
            deg = jax.ops.segment_sum(jnp.ones_like(dst, dtype=x.dtype), dst, num_segments=n)
            dinv = jnp.where(deg > 0, jax.lax.rsqrt(deg), 0.0)
            norm = dinv[src] * dinv[dst]
            msg = xw[src] * norm[:, None]
            out = jax.ops.segment_sum(msg, dst, num_segments=n)
            return out + b
        h = gcn_conv(x.astype(jnp.float32), edge_index, W1, b1)
        h = jax.nn.relu(h)
        h = gcn_conv(h, edge_index, W2, b2)
        return jax.nn.relu(h)

    def _L1_gnn_ref(x, edge_index, W, att_src, att_dst, bias, ln_w, ln_b, prelu_w):
        import jax, jax.numpy as jnp
        import numpy as np
        N = 50000
        E = 25000
        IN = 128
        H = 4
        C = 32
        OUT = H * C
        NEG_SLOPE = 0.2
        LN_EPS = 1e-05
        n = x.shape[0]
        h = (x @ W).reshape(n, H, C)
        a_s = jnp.einsum('nhc,hc->nh', h, att_src)
        a_d = jnp.einsum('nhc,hc->nh', h, att_dst)
        loops = jnp.arange(n, dtype=edge_index.dtype)
        src = jnp.concatenate([edge_index[0], loops])
        dst = jnp.concatenate([edge_index[1], loops])
        e = jax.nn.leaky_relu(a_s[src] + a_d[dst], NEG_SLOPE)
        m = jax.ops.segment_max(e, dst, num_segments=n)
        p = jnp.exp(e - m[dst])
        denom = jax.ops.segment_sum(p, dst, num_segments=n)
        alpha = p / (denom[dst] + 1e-16)
        out = jax.ops.segment_sum(h[src] * alpha[:, :, None], dst, num_segments=n)
        out = out.reshape(n, H * C) + bias
        mu = jnp.mean(out, axis=-1, keepdims=True)
        var = jnp.var(out, axis=-1, keepdims=True)
        y = (out - mu) * jax.lax.rsqrt(var + LN_EPS) * ln_w + ln_b
        return jnp.where(y >= 0, y, prelu_w * y)

    def _L2_gnn_ref(og_x, edge_index, edge_weight, W, att_l, att_r, W_res):
        import jax, jax.numpy as jnp
        import numpy as np
        N_NODES = 50000
        N_EDGES = 50000
        IN_DIM = 128
        N_HEADS = 8
        OUT_DIM = 128
        HEAD_DIM = OUT_DIM // N_HEADS
        N = og_x.shape[0]
        src, dst = (edge_index[0], edge_index[1])
        x = (og_x @ W).reshape(N, N_HEADS, HEAD_DIM)
        alpha_l = jnp.sum(x * att_l, axis=-1)
        alpha_r = jnp.sum(x * att_r, axis=-1)
        alpha = alpha_l[src] + alpha_r[dst]
        alpha = edge_weight[:, None] * alpha
        alpha = jax.nn.leaky_relu(alpha, negative_slope=0.2)
        seg_max = jax.ops.segment_max(alpha, dst, num_segments=N)
        seg_max = jnp.where(jnp.isfinite(seg_max), seg_max, 0.0)
        exp_a = jnp.exp(alpha - seg_max[dst])
        seg_sum = jax.ops.segment_sum(exp_a, dst, num_segments=N)
        coef = exp_a / (seg_sum[dst] + 1e-16)
        msg = x[src] * coef[:, :, None]
        agg = jax.ops.segment_sum(msg, dst, num_segments=N)
        out = jax.nn.elu(agg).reshape(N, N_HEADS * HEAD_DIM)
        out = out + og_x @ W_res
        return out

    def _L3_gnn_ref(x, edge_index, ln1_g, ln1_b, W, att_src, att_dst, gat_b, ln2_g, ln2_b, w1, b1, w2, b2):
        import jax, jax.numpy as jnp
        import numpy as np
        N = 50000
        E = 25000
        DIN = 128
        H = 4
        C = 32
        EPS = 1e-05
        NEG_SLOPE = 0.2

        def layer_norm(x, g, b):
            m = jnp.mean(x, axis=-1, keepdims=True)
            v = jnp.mean((x - m) ** 2, axis=-1, keepdims=True)
            return (x - m) * jax.lax.rsqrt(v + EPS) * g + b

        def gat_conv(h, src, dst, W, att_src, att_dst, gat_b, n):
            xh = (h @ W).reshape(n, H, C)
            a_src = jnp.einsum('nhc,hc->nh', xh, att_src)
            a_dst = jnp.einsum('nhc,hc->nh', xh, att_dst)
            alpha = jax.nn.leaky_relu(a_src[src] + a_dst[dst], NEG_SLOPE)
            amax = jax.ops.segment_max(alpha, dst, num_segments=n)
            alpha = jnp.exp(alpha - amax[dst])
            denom = jax.ops.segment_sum(alpha, dst, num_segments=n)
            alpha = alpha / denom[dst]
            msg = xh[src] * alpha[:, :, None]
            out = jax.ops.segment_sum(msg, dst, num_segments=n)
            return out.reshape(n, H * C) + gat_b
        n = x.shape[0]
        loops = jnp.arange(n, dtype=edge_index.dtype)
        src = jnp.concatenate([edge_index[0], loops])
        dst = jnp.concatenate([edge_index[1], loops])
        h = layer_norm(x, ln1_g, ln1_b)
        h = gat_conv(h, src, dst, W, att_src, att_dst, gat_b, n)
        h = h + x
        hn = layer_norm(h, ln2_g, ln2_b)
        ffn = jax.nn.gelu(hn @ w1 + b1, approximate=False) @ w2 + b2
        return h + ffn
    edge_index = jnp.stack([src, dst])
    x = _layernorm(x + _L0_gnn_ref(x, edge_index, L0_gnn_W1, L0_gnn_b1, L0_gnn_W2, L0_gnn_b2), axis=-1)
    x = _layernorm(x + _L1_gnn_ref(x, edge_index, L1_gnn_W, L1_gnn_att_src, L1_gnn_att_dst, L1_gnn_bias, L1_gnn_ln_w, L1_gnn_ln_b, L1_gnn_prelu_w), axis=-1)
    x = _layernorm(x + _L2_gnn_ref(x, edge_index, edge_weight, L2_gnn_W, L2_gnn_att_l, L2_gnn_att_r, L2_gnn_W_res), axis=-1)
    x = _layernorm(x + _L3_gnn_ref(x, edge_index, L3_gnn_ln1_g, L3_gnn_ln1_b, L3_gnn_W, L3_gnn_att_src, L3_gnn_att_dst, L3_gnn_gat_b, L3_gnn_ln2_g, L3_gnn_ln2_b, L3_gnn_w1, L3_gnn_b1, L3_gnn_w2, L3_gnn_b2), axis=-1)
    return x

_drawn_inputs = setup_inputs


def setup_inputs(seed=0):
    import zlib

    import numpy as np

    out = dict(_drawn_inputs(seed))
    spreads = {'L0_gnn_b1': (0.0, 0.1),
     'L0_gnn_b2': (0.0, 0.1),
     'L1_gnn_ln_w': (1.0, 0.2),
     'L1_gnn_ln_b': (0.0, 0.1),
     'L3_gnn_ln1_g': (1.0, 0.2),
     'L3_gnn_ln1_b': (0.0, 0.1),
     'L3_gnn_gat_b': (0.0, 0.1),
     'L3_gnn_ln2_g': (1.0, 0.2),
     'L3_gnn_ln2_b': (0.0, 0.268),
     'L3_gnn_b1': (0.0, 0.1),
     'L3_gnn_b2': (0.0, 0.1)}
    factors = {'L0_gnn_W1': 5.247, 'L2_gnn_att_r': 2.843}
    for name, (base, spread) in spreads.items():
        noise = np.random.default_rng([zlib.crc32(name.encode()), seed]).standard_normal(out[name].shape)
        drawn = base * np.exp(spread * noise) if base else spread * noise
        out[name] = jnp.asarray(drawn.astype(out[name].dtype))
    for name, factor in factors.items():
        out[name] = (out[name] * factor).astype(out[name].dtype)
    return out
```

```python
from contextlib import ExitStack

import concourse.bass as bass
from concourse import mybir

F32 = mybir.dt.float32
I32 = mybir.dt.int32
ALU = mybir.AluOpType
ACT = mybir.ActivationFunctionType
AX = mybir.AxisListType

P = 128
N = 3125
E = 100000
F = 128
NODE_TILES = -(-N // P)
NPAD = NODE_TILES * P
EDGE_TILES = -(-E // P)
EPAD = EDGE_TILES * P
UNIT_TILES = EDGE_TILES // 2
REAL_STEPS = 2 * (UNIT_TILES + NODE_TILES - 1)
U = 16
UNITS = U // 2
PAIRS = -(-REAL_STEPS // (2 * U))
STEPS = PAIRS * 2 * U
G = -(-STEPS // P)
LANES = G * P
NEG = -1.0e30
PER_BANK = 3
BANKS = -(-UNITS // PER_BANK)
BLK = 5
assert NODE_TILES % BLK == 0 and EDGE_TILES % 2 == 0 and STEPS <= LANES and 2 * BANKS <= 8


class Chain:

    def __init__(self, eng, sem):
        self.eng, self.sem, self.n = eng, sem, 0

    def __call__(self, ins):
        self.n += 1
        ins.then_inc(self.sem, 1)
        self.eng.wait_ge(self.sem, self.n)


def over(ap, shape):
    return ap.to_broadcast(shape)


class Net:
    pass


class Phase:

    used = []
    count = 0

    def __init__(self, nc):
        self.nc = nc

    def __enter__(self):
        return self

    def __exit__(self, *error):
        return False

    def semaphore(self, name):
        sem = self.nc.alloc_semaphore(f"{name}_{Phase.count}")
        Phase.used.append(sem)
        Phase.count += 1
        return sem


def phase(nc, *names):
    ph = Phase(nc)
    return ph, [ph.semaphore(n) for n in names]


def end_of_layer(nc):
    nc.all_engine_barrier()
    nc.clear_and_free_semaphores(Phase.used)
    Phase.used = []
    nc.all_engine_barrier()


def allocate(nc, ctx, m):
    def sb(name, shape, dt=F32):
        return ctx.enter_context(nc.sbuf_tensor(name, shape, dt))

    m.iota = sb("iota_row", [P, P])
    m.ident = sb("identity", [P, P])
    m.x = sb("node_x", [P, NODE_TILES, F])
    m.tab = sb("node_table", [P, NODE_TILES, F + 8])
    m.acc = sb("node_sums", [P, NODE_TILES, F + 8])
    m.drel = sb("lane_dst_rel", [P, LANES])
    m.src = sb("lane_src", [P, LANES], I32)
    m.jrow = sb("unit_node_tile", [1, LANES // 2], I32)
    m.keep = sb("step_keep", [P, G, P])
    m.valid = sb("step_valid", [P, G, P])
    m.nostart = sb("step_nostart", [P, G, P])
    m.lane = sb("lane_coef", [P, LANES, 8])
    m.big = sb("work", [P, 3 * 8 * LANES])
    m.last_all = None
    m.carry = [sb(f"carry{i}", [8, LANES + 1]) for i in range(2)]
    m.dinv = sb("node_dinv", [P, NODE_TILES])
    m.has = sb("node_has_edges", [P, NODE_TILES])
    m.pos_first = sb("node_pos_first", [P, NODE_TILES], I32)
    m.pos_last = sb("node_pos_last", [P, NODE_TILES], I32)
    m.a_src = sb("node_a_src", [P, NODE_TILES, 8])
    m.a_dst = sb("node_a_dst", [P, NODE_TILES, 8])
    m.self_a = sb("node_self_alpha", [P, NODE_TILES, 8])
    m.node_m = sb("node_max", [P, NODE_TILES, 8])
    m.stat = [sb(f"node_stat{i}", [P, NODE_TILES]) for i in range(4)]
    m.node_no = sb("node_number", [P, NODE_TILES])
    m.step_no = sb("step_number", [P, G], I32)
    m.step_tile = sb("step_edge_tile", [P, G], I32)
    m.step_base = sb("step_node_base", [P, G])
    m.open_row = sb("row_nostart", [8, LANES])
    m.step_carry = sb("step_carry", [P, G, 8])
    m.idx_row = sb("step_j_rows", [8, P], I32)
    m.j_regs = [nc.vector.alloc_register(f"unit_j{k}") for k in range(UNITS)]
    m.weights = {}
    R = U * (F + 8)
    big = m.big
    m.ring = [big[:, h * R:(h + 1) * R] for h in range(2)]
    m.msg = [big[:, (2 + h) * R:(3 + h) * R] for h in range(2)]
    m.onehot = [big[:, 4 * R + h * U * P:4 * R + (h + 1) * U * P].rearrange("p (u d) -> p u d", d=P) for h in range(2)]
    base = 4 * R + 2 * U * P
    m.idx = [sb(f"gather_index{h}", [P, U], I32) for h in range(2)]
    W = NODE_TILES * F
    m.node = [big[:, lo:lo + W].rearrange("p (j f) -> p j f", f=F) for lo in (base, base + W, 6 * BLK * P)]
    assert base + 2 * W <= 3 * 8 * LANES and 6 * BLK * P + W <= base

    m.ps = [ctx.enter_context(nc.psum_tensor(f"psum{i}", [P, 1024], F32)) for i in range(4)]

    def dram(name, shape, dt=F32):
        return nc.dram_tensor(name, shape, dt, kind="Internal").ap()

    m.d_table = {H: dram(f"table_{H}", [NPAD, F + H]) for H in (0, 4, 8)}
    m.d_rows = {H: dram(f"rows_{H}", [P, STEPS, F + H]) for H in (4, 8)}
    m.d_spread = {H: dram(f"spread_{H}", [LANES * P + NPAD, H]) for H in (4, 8)}
    m.d_max = {H: dram(f"edge_max_{H}", [LANES * P, H]) for H in (4, 8)}
    m.d_j = dram("unit_j", [G, P // 2], I32)
    m.d_ptr = dram("row_ptr", [NPAD + 1, 1])


def load_parameters(nc, ctx, m, a):
    vectors = ["L0_gnn_b2", "L1_gnn_att_src", "L1_gnn_att_dst", "L1_gnn_bias", "L1_gnn_ln_w",
               "L1_gnn_ln_b", "L1_gnn_prelu_w", "L2_gnn_att_l", "L2_gnn_att_r", "L3_gnn_ln1_g",
               "L3_gnn_ln1_b", "L3_gnn_att_src", "L3_gnn_att_dst", "L3_gnn_gat_b", "L3_gnn_ln2_g",
               "L3_gnn_ln2_b", "L3_gnn_b2"]
    plain = ["L0_W1T", "L0_b1T", "L1_gnn_W", "L2_gnn_W", "L2_gnn_W_res", "L3_gnn_W", "L3_gnn_w1", "L3_b1T"]
    halves = ["L0_W2T", "L3_gnn_w2"]
    w = m.weights
    for n in vectors:
        w[n] = ctx.enter_context(nc.sbuf_tensor("w_" + n, [P, a[n].shape[1]], F32))
    for n in plain:
        w[n] = ctx.enter_context(nc.sbuf_tensor("w_" + n, [P, a[n].shape[1]], F32))
    for n in halves:
        w[n] = ctx.enter_context(nc.sbuf_tensor("w_" + n, [P, a[n].shape[0] // P, F], F32))
    ph, (loaded, iota_done, zeroed) = phase(nc, "params_loaded", "iota_done", "zeroed")
    with ph, nc.Block() as block:
        @block.sync
        def _(sp):
            sp.dma_start(m.x[:], a["x"].rearrange("(j p) f -> p j f", p=P)).then_inc(loaded, 16)
            for n in vectors:
                sp.dma_start(w[n][:], over(a[n], [P, a[n].shape[1]])).then_inc(loaded, 16)
            for n in plain:
                sp.dma_start(w[n][:], a[n]).then_inc(loaded, 16)
            for n in halves:
                sp.dma_start(w[n][:], a[n].rearrange("(c p) f -> p c f", p=P)).then_inc(loaded, 16)
            sp.wait_ge(zeroed, 1)
            for H in (4, 8):
                sp.dma_start(m.d_spread[H][0:LANES * P, :].rearrange("(p r) h -> p (r h)", p=P),
                             m.big[:, 0:LANES * H]).then_inc(loaded, 16)
            sp.wait_ge(loaded, 16 * (3 + len(vectors) + len(plain) + len(halves)))

        @block.gpsimd
        def _(pool):
            chain = Chain(pool, iota_done)
            chain(pool.iota(m.iota[:], [[1, P]], base=0, channel_multiplier=0, allow_small_or_imprecise_dtypes=True))
            chain(pool.iota(m.node_no[:], [[P, NODE_TILES]], base=0, channel_multiplier=1, allow_small_or_imprecise_dtypes=True))
            chain(pool.iota(m.step_no[:], [[P, G]], base=0, channel_multiplier=1))
            chain(pool.iota(m.carry[0][0:1, 0:EDGE_TILES], [[1, EDGE_TILES]], base=1, channel_multiplier=0,
                            allow_small_or_imprecise_dtypes=True))
            chain(pool.memset(m.ident[:], 0.0))
            chain(pool.affine_select(out=m.ident[:], in_=m.ident[:], compare_op=ALU.not_equal, fill=1.0,
                                     base=0, pattern=[[-1, P]], channel_multiplier=1))

        @block.vector
        def _(dve):
            dve.memset(m.big[:, 0:8 * LANES], 0.0).then_inc(zeroed, 1)
            dve.memset(m.lane[:], 0.0)



def ge(ap):
    return ap.rearrange("p g e -> p (g e)")


def step_tables(nc, m, a):
    T, T2 = EDGE_TILES, UNIT_TILES
    rows = [m.big[:, i * T:(i + 1) * T] for i in range(6)]
    last_i, last_f, begin, begin_all, hit, spare = rows
    at = 6 * T
    unit, odd, t_of, j_of, j_cap, unit_i, odd_i = (m.big[:, at + i * G:at + (i + 1) * G] for i in range(7))
    at += 7 * G
    ones = m.big[:, at:at + P]
    m.last_all = m.tab[:].rearrange("p j f -> p (j f)")[:, 0:T]
    ph, (loaded, dve_step, spread, tiles_known, turned, stored) = phase(
        nc, "loaded", "dve_step", "rows_spread", "tiles_known", "j_turned", "j_stored")
    ps_begin = m.ps[0]
    ps_last = m.ps[1]
    ps_j = m.ps[2]
    with ph, nc.Block() as block:

        @block.sync
        def _(sp):
            sp.dma_start(last_i[0:1, :].bitcast(I32), a["tile_last"]).then_inc(loaded, 16)
            sp.wait_ge(tiles_known, 2)
            sp.dma_start(m.d_j, m.idx_row[0:G, 0:P // 2]).then_inc(stored, 16)
            sp.wait_ge(stored, 16)
            sp.dma_start(m.jrow[:], m.d_j.rearrange("(a g) p -> a (g p)", a=1)).then_inc(stored, 16)
            sp.wait_ge(stored, 32)

        @block.tensor
        def _(pe):
            pe.wait_ge(dve_step, 5)
            for row, out, n in ((begin, ps_begin, T2), (last_f, ps_last, T)):
                for lo in range(0, n, 512):
                    hi = min(lo + 512, n)
                    pe.matmul(out[:, lo:hi], ones[0:1, :], row[0:1, lo:hi], start=True, stop=True).then_inc(spread, 1)
            pe.wait_ge(tiles_known, 1)
            pe.transpose(ps_j[0:G, 0:P], j_cap, m.ident[:]).then_inc(turned, 1)

        @block.vector
        def _(dve):
            chain = Chain(dve, dve_step)
            chain(dve.memset(ones, 1.0))
            dve.wait_ge(loaded, 16)
            chain(dve.tensor_scalar(spare[0:1, :].bitcast(I32), last_i[0:1, :].bitcast(I32), 7, None, ALU.logical_shift_right))
            chain(dve.tensor_copy(hit[0:1, :], spare[0:1, :].bitcast(I32)))
            chain(dve.tensor_copy(last_f[0:1, :], last_i[0:1, :].bitcast(I32)))
            chain(dve.tensor_tensor(begin[0:1, 0:T2], hit[0:1, 1:T:2], m.carry[0][0:1, 0:T2], ALU.add))
            chain(dve.tensor_scalar(unit_i.bitcast(I32), m.step_no[:], 1, None, ALU.logical_shift_right))
            chain(dve.tensor_scalar(odd_i.bitcast(I32), m.step_no[:], 1, None, ALU.bitwise_and))
            chain(dve.tensor_copy(unit, unit_i.bitcast(I32)))
            chain(dve.tensor_copy(odd, odd_i.bitcast(I32)))
            dve.wait_ge(spread, 3)
            chain(dve.tensor_copy(begin_all[:, 0:T2], ps_begin[:, 0:T2]))
            chain(dve.tensor_copy(m.last_all, ps_last[:, 0:T]))
            for g in range(G):
                chain(dve.tensor_scalar(hit[:, 0:T2 - 1], begin_all[:, 0:T2 - 1], unit[:, g:g + 1], None, ALU.is_le))
                chain(dve.tensor_reduce(t_of[:, g:g + 1], hit[:, 0:T2 - 1], AX.X, ALU.add))
            chain(dve.tensor_tensor(j_of, unit, t_of, ALU.subtract))
            chain(dve.scalar_tensor_tensor(out=unit, in0=t_of, scalar=2.0, in1=odd, op0=ALU.mult, op1=ALU.add))
            chain(dve.tensor_copy(m.step_tile[:], unit))
            chain(dve.tensor_scalar(m.step_base[:], j_of, float(P), None, ALU.mult))
            chain(dve.tensor_scalar(j_cap, j_of, float(NODE_TILES - 1), None, ALU.min))
            dve.engine_nop().then_inc(tiles_known, 1)
            dve.wait_ge(turned, 1)
            dve.tensor_copy(m.idx_row[0:G, 0:P // 2], ps_j[0:G, 0:P:2]).then_inc(tiles_known, 1)


def step_edges(nc, m, a):
    def part(i):
        return m.big[:, i * LANES:(i + 1) * LANES].rearrange("p (g e) -> p g e", e=P)

    names = ("dst", "dst_before", "src")
    raw = {n: part(i).bitcast(I32) for i, n in enumerate(names)}
    dst, before, src = part(3), part(4), part(5)
    start, rel = part(6), part(7)
    ph, (gathered, dve_step, rel_known, turned) = phase(nc, "edges_gathered", "dve_step", "rel_known", "edges_turned")
    ps_rel = m.ps[0]
    ps_src = m.ps[1]
    ps_open = m.ps[2]
    with ph, nc.Block() as block:

        @block.gpsimd
        def _(pool):
            for n in names:
                for g in range(G):
                    pool.indirect_dma_start(raw[n][:, g, :], None, a[n],
                                            bass.IndirectOffsetOnAxis(ap=m.step_tile[:, g:g + 1], axis=0)).then_inc(gathered, 16)

        @block.tensor
        def _(pe):
            pe.wait_ge(rel_known, 1)
            for g in range(G):
                pe.transpose(ps_rel[:, g * P:(g + 1) * P], rel[:, g, :], m.ident[:]).then_inc(turned, 1)
                pe.transpose(ps_src[:, g * P:(g + 1) * P], src[:, g, :], m.ident[:]).then_inc(turned, 1)
            pe.wait_ge(rel_known, 2)
            for g in range(G):
                pe.transpose(ps_open[0:8, g * P:(g + 1) * P], m.step_carry[:, g, :], m.ident[:]).then_inc(turned, 1)

        @block.vector
        def _(dve):
            chain = Chain(dve, dve_step)
            dve.wait_ge(gathered, 16 * 3 * G)
            chain(dve.tensor_copy(dst, raw["dst"]))
            chain(dve.tensor_copy(before, raw["dst_before"]))
            chain(dve.tensor_copy(src, raw["src"]))
            chain(dve.tensor_tensor(rel, dst, over(m.step_base[:].unsqueeze(2), [P, G, P]), ALU.subtract))
            dve.engine_nop().then_inc(rel_known, 1)
            chain(dve.tensor_scalar(m.valid[:], rel, 0.0, None, ALU.is_ge))
            chain(dve.tensor_scalar(m.nostart[:], rel, float(P), None, ALU.is_lt))
            chain(dve.tensor_tensor(m.valid[:], m.valid[:], m.nostart[:], ALU.mult))
            chain(dve.tensor_tensor(start, dst, before, ALU.not_equal))
            chain(dve.tensor_tensor(start, start, m.valid[:], ALU.mult))
            chain(dve.tensor_scalar(m.keep[:], start, -1.0, 1.0, ALU.mult, ALU.add))
            chain(dve.memset(m.keep[:, :, 0:1], 0.0))
            chain(dve.tensor_tensor_scan(ge(before), ge(m.keep[:]), ge(start), 0.0, ALU.mult, ALU.add))
            chain(dve.tensor_scalar(m.nostart[:], before, -1.0, 1.0, ALU.mult, ALU.add))
            chain(dve.tensor_copy(m.step_carry[:], over(m.nostart[:, :, P - 1:P], [P, G, 8])))
            dve.engine_nop().then_inc(rel_known, 1)
            dve.wait_ge(turned, 3 * G)
            chain(dve.tensor_copy(m.drel[:], ps_rel[:, 0:LANES]))
            chain(dve.tensor_copy(m.src[:], ps_src[:, 0:LANES]))
            chain(dve.tensor_copy(m.open_row[:], ps_open[0:8, 0:LANES]))


def row_pointers(nc, m, a):
    T = EDGE_TILES
    JP = NODE_TILES * P
    rows_i = m.big[:, 0:JP].bitcast(I32).rearrange("p (j e) -> p j e", e=P)
    rows = m.big[:, JP:2 * JP].rearrange("p (j e) -> p j e", e=P)
    hit = m.big[:, 2 * JP:2 * JP + T]
    at = 2 * JP + T
    tiles_before, in_tile, ptr, ptr_next, s0, s1, s2 = (m.big[:, at + i * NODE_TILES:at + (i + 1) * NODE_TILES] for i in range(7))
    at += 7 * NODE_TILES
    ptr_row, next_row, last = (m.big[:, at + i * P:at + (i + 1) * P] for i in range(3))
    tiles_int = m.pos_first
    ph, (dve_step, tiles_known, gathered, ptr_known, turned, row_known, stored, loaded, deg_known, root) = phase(
        nc, "dve_step", "tiles_known", "rows_gathered", "ptr_known", "ptr_turned", "row_known", "ptr_stored",
        "next_loaded", "degree_known", "root_done")
    ps_row = m.ps[0]
    ps_next = m.ps[1]
    with ph, nc.Block() as block:

        @block.sync
        def _(sp):
            sp.wait_ge(row_known, 1)
            sp.dma_start(m.d_ptr[0:NPAD, :].rearrange("(j p) a -> j (p a)", p=P), ptr_row[0:NODE_TILES, :]).then_inc(stored, 16)
            sp.dma_start(m.d_ptr[NPAD:NPAD + 1, :], last[0:1, 0:1]).then_inc(stored, 16)
            sp.wait_ge(stored, 32)
            sp.dma_start(next_row[0:NODE_TILES, :], m.d_ptr[1:NPAD + 1, :].rearrange("(j p) a -> j (p a)", p=P)).then_inc(loaded, 16)

        @block.gpsimd
        def _(pool):
            pool.wait_ge(tiles_known, 1)
            for j in range(NODE_TILES):
                pool.indirect_dma_start(rows_i[:, j, :], None, a["dst"],
                                        bass.IndirectOffsetOnAxis(ap=tiles_int[:, j:j + 1], axis=0)).then_inc(gathered, 16)

        @block.tensor
        def _(pe):
            pe.wait_ge(ptr_known, 1)
            pe.transpose(ps_row[0:NODE_TILES, 0:P], ptr, m.ident[:]).then_inc(turned, 1)
            pe.wait_ge(loaded, 16)
            pe.transpose(ps_next[:, 0:NODE_TILES], next_row[0:NODE_TILES, :],
                         m.ident[0:NODE_TILES, 0:NODE_TILES]).then_inc(turned, 1)

        @block.scalar
        def _(act):
            act.wait_ge(deg_known, 1)
            act.activation(s2, s0, ACT.Sqrt).then_inc(root, 1)

        @block.vector
        def _(dve):
            chain = Chain(dve, dve_step)
            for j in range(NODE_TILES):
                chain(dve.tensor_scalar(hit, m.last_all, m.node_no[:, j:j + 1], None, ALU.is_lt))
                chain(dve.tensor_reduce(tiles_before[:, j:j + 1], hit, AX.X, ALU.add))
            dve.tensor_copy(tiles_int[:], tiles_before).then_inc(tiles_known, 1)
            chain(dve.memset(last[0:1, :], float(EPAD)))
            dve.wait_ge(gathered, 16 * NODE_TILES)
            chain(dve.tensor_copy(rows, rows_i))
            chain(dve.tensor_tensor(rows, rows, over(m.node_no[:].unsqueeze(2), [P, NODE_TILES, P]), ALU.is_lt))
            chain(dve.tensor_reduce(in_tile, rows, AX.X, ALU.add))
            chain(dve.tensor_scalar(ptr, tiles_before, float(P), None, ALU.mult))
            chain(dve.tensor_tensor(ptr, ptr, in_tile, ALU.add))
            dve.engine_nop().then_inc(ptr_known, 1)
            dve.wait_ge(turned, 1)
            dve.tensor_copy(ptr_row[0:NODE_TILES, :], ps_row[0:NODE_TILES, 0:P]).then_inc(row_known, 1)
            dve.wait_ge(turned, 2)
            chain(dve.tensor_copy(ptr_next, ps_next[:, 0:NODE_TILES]))
            chain(dve.tensor_tensor(s0, ptr_next, ptr, ALU.subtract))
            chain(dve.tensor_scalar(m.has[:], s0, 1.0, None, ALU.min))
            chain(dve.tensor_scalar(s1, s0, 1.0, None, ALU.add))
            chain(dve.reciprocal(s0, s1))
            dve.engine_nop().then_inc(deg_known, 1)
            dve.wait_ge(root, 1)
            chain(dve.tensor_tensor(s0, s2, s2, ALU.mult))
            chain(dve.tensor_tensor(s0, s0, s1, ALU.mult))
            chain(dve.tensor_scalar(s0, s0, -0.5, 1.5, ALU.mult, ALU.add))
            chain(dve.tensor_tensor(m.dinv[:], s0, s2, ALU.mult))
            chain(dve.tensor_scalar(s0, m.node_no[:], m.node_no[:, 0:1], 2.0, ALU.subtract, ALU.mult))
            chain(dve.tensor_tensor(ptr, ptr, s0, ALU.add))
            chain(dve.tensor_scalar(ptr_next, ptr_next, -1.0, 0.0, ALU.add, ALU.max))
            chain(dve.tensor_tensor(ptr_next, ptr_next, s0, ALU.add))
            chain(dve.tensor_copy(m.pos_last[:], ptr_next))
            chain(dve.tensor_scalar(s1, m.node_no[:], float(LANES * P), None, ALU.add))
            chain(dve.tensor_tensor(ptr, ptr, s1, ALU.subtract))
            chain(dve.tensor_tensor(ptr, ptr, m.has[:], ALU.mult))
            chain(dve.tensor_tensor(ptr, ptr, s1, ALU.add))
            chain(dve.tensor_copy(m.pos_first[:], ptr))


def store_table(nc, m, H, parts):
    ph, (stored,) = phase(nc, "table_stored")
    with ph, nc.Block(no_gpsimd_drain=True) as block:
        @block.sync
        def _(sp):
            for view, lo, hi in parts:
                sp.dma_start(m.d_table[H].rearrange("(j p) f -> p j f", p=P)[:, :, lo:hi], view).then_inc(stored, 16)
            sp.wait_ge(stored, 16 * len(parts))


def gather_half(pool, m, H, i, h, copied):
    at = i * (2 * U) + h * U
    pool.tensor_copy(m.idx[h][:], m.src[:, bass.ds(at, U)]).then_inc(copied, 1)
    pool.wait_ge(copied, 2 * i + h + 1)
    pool.nop(nofuse=True)
    W = F + H
    for k in range(U):
        yield pool.indirect_dma_start(m.ring[h][:, k * W:(k + 1) * W], None, m.d_table[H],
                                      bass.IndirectOffsetOnAxis(ap=m.idx[h][:, k:k + 1], axis=0))


def gather_rows(nc, m, H):
    W = F + H
    ph, (copied, got0, got1, kept0, kept1, taken) = phase(
        nc, "index_copied", "rows_in_0", "rows_in_1", "rows_out_0", "rows_out_1", "columns_taken")
    got, out = (got0, got1), (kept0, kept1)
    with ph, nc.Block() as block:

        @block.gpsimd
        def _(pool):
            def half(i, h, first):
                if not first:
                    pool.wait_ge(out[h], 16 * i)
                    pool.wait_ge(taken, 2 * i + h - 1)
                for dma in gather_half(pool, m, H, i, h, copied):
                    dma.then_inc(got[h], 16)

            half(0, 0, True)
            half(0, 1, True)
            with pool.Fori(1, PAIRS) as i:
                half(i, 0, False)
                half(i, 1, False)

        @block.sync
        def _(sp):
            with sp.Fori(0, PAIRS) as i:
                for h in range(2):
                    sp.wait_ge(got[h], (i + 1) * (16 * U))
                    sp.dma_start(m.d_rows[H][:, bass.ds(i * (2 * U) + h * U, U), :].rearrange("e s f -> e (s f)"),
                                 m.ring[h][:, 0:U * W]).then_inc(out[h], 16)
            for h in range(2):
                sp.wait_ge(out[h], 16 * PAIRS)

        @block.scalar
        def _(act):
            with act.Fori(0, PAIRS) as i:
                for h in range(2):
                    act.wait_ge(got[h], (i + 1) * (16 * U))
                    rows = m.ring[h][:, 0:U * W].rearrange("p (u f) -> p u f", f=W)
                    act.copy(m.lane[:, bass.ds(i * (2 * U) + h * U, U), 0:H], rows[:, :, F:W]).then_inc(taken, 1)


def sum_edges(nc, m, H):
    W = F + H
    C = F // H if H else F
    names = ("index_copied", "rows_in_0", "rows_in_1", "onehot_done", "messages_done", "product_done",
             "sum_done", "tails_done", "cleared")
    ph, (copied, got0, got1, hot_done, msg_done, prod, summed, tails, cleared) = phase(nc, *names)
    got = (got0, got1)

    def at(i, h):
        return i * (2 * U) + h * U

    with ph, nc.Block() as block:
        def out(h, k):
            bank = h * BANKS + k // PER_BANK
            at = bank % 2 * 512 + (k % PER_BANK) * W
            return m.ps[bank // 2][:, at:at + W]

        if H == 0:
            @block.gpsimd
            def _(pool):
                def half(i, h, first):
                    if not first:
                        pool.wait_ge(prod, UNITS * (2 * i + h - 1))
                    for dma in gather_half(pool, m, 0, i, h, copied):
                        dma.then_inc(got[h], 16)

                half(0, 0, True)
                half(0, 1, True)
                with pool.Fori(1, PAIRS) as i:
                    half(i, 0, False)
                    half(i, 1, False)
        else:
            @block.sync
            def _(sp):
                def half(i, h, first):
                    if not first:
                        sp.wait_ge(msg_done, 2 * i + h - 1)
                    sp.dma_start(m.ring[h][:, 0:U * W], m.d_rows[H][:, bass.ds(at(i, h), U), :].rearrange("e s f -> e (s f)")
                                 ).then_inc(got[h], 16)

                half(0, 0, True)
                half(0, 1, True)
                with sp.Fori(1, PAIRS) as i:
                    half(i, 0, False)
                    half(i, 1, False)

            @block.gpsimd
            def _(pool):
                def half(i, h, first):
                    pool.wait_ge(got[h], (i + 1) * 16)
                    if not first:
                        pool.wait_ge(prod, UNITS * (2 * i + h - 1))
                    rows = m.ring[h][:, 0:U * W].rearrange("p (u f) -> p u f", f=W)[:, :, 0:F]
                    to = m.msg[h][:, 0:U * W].rearrange("p (u f) -> p u f", f=W)[:, :, 0:F]
                    coef = m.lane[:, bass.ds(at(i, h), U), 0:H]
                    pool.tensor_tensor(to.rearrange("p u (h c) -> p u h c", c=C), rows.rearrange("p u (h c) -> p u h c", c=C),
                                       over(coef.unsqueeze(3), [P, U, H, C]), ALU.mult).then_inc(msg_done, 1)

                half(0, 0, True)
                half(0, 1, True)
                with pool.Fori(1, PAIRS) as i:
                    half(i, 0, False)
                    half(i, 1, False)

            @block.scalar
            def _(act):
                def half(i, h, first):
                    if not first:
                        act.wait_ge(prod, UNITS * (2 * i + h - 1))
                    to = m.msg[h][:, 0:U * W].rearrange("p (u f) -> p u f", f=W)[:, :, F:W]
                    act.copy(to, m.lane[:, bass.ds(at(i, h), U), 0:H]).then_inc(tails, 1)

                half(0, 0, True)
                half(0, 1, True)
                with act.Fori(1, PAIRS) as i:
                    half(i, 0, False)
                    half(i, 1, False)

        @block.tensor
        def _(pe):
            def half(i, h, first):
                n = 2 * i + h
                pe.wait_ge(hot_done, n + 1)
                if H:
                    pe.wait_ge(msg_done, n + 1)
                    pe.wait_ge(tails, n + 1)
                else:
                    pe.wait_ge(got[h], (i + 1) * (16 * U))
                if not first:
                    pe.wait_ge(summed, UNITS * (n - 1))
                src = m.msg[h] if H else m.ring[h]
                for k in range(U):
                    mm = pe.matmul(out(h, k // 2), m.onehot[h][:, k, :], src[:, k * W:(k + 1) * W], start=(k % 2 == 0), stop=(k % 2 == 1))
                    if k % 2:
                        mm.then_inc(prod, 1)

            half(0, 0, True)
            half(0, 1, True)
            with pe.Fori(1, PAIRS) as i:
                half(i, 0, False)
                half(i, 1, False)

        @block.vector
        def _(dve):
            def onehot(i, h, first):
                if not first:
                    dve.wait_ge(prod, UNITS * (2 * i + h - 1))
                dve.tensor_tensor(m.onehot[h], over(m.iota[:].unsqueeze(1), [P, U, P]),
                                  over(m.drel[:, bass.ds(at(i, h), U)].unsqueeze(2), [P, U, P]), ALU.is_equal).then_inc(hot_done, 1)

            def add_up(i, h):
                n = i * (2 * UNITS) + h * UNITS
                dve.load(m.j_regs, m.jrow[0:1, bass.ds(n, UNITS)])
                for k in range(UNITS):
                    j = dve.snap(m.j_regs[k], min_val=0, max_val=NODE_TILES - 1)
                    if k % PER_BANK == 0:
                        dve.wait_ge(prod, n + min(k + PER_BANK, UNITS))
                    if not (isinstance(n, int) and n + k == 0):
                        dve.wait_ge(summed, n + k)
                    sums = m.acc[:, bass.ds(j, 1), 0:W].rearrange("p a f -> p (a f)")
                    dve.tensor_tensor(sums, sums, out(h, k), ALU.add).then_inc(summed, 1)

            dve.memset(m.acc[:], 0.0).then_inc(cleared, 1)
            dve.wait_ge(cleared, 1)
            onehot(0, 0, True)
            onehot(0, 1, True)
            add_up(0, 0)
            with dve.Fori(1, PAIRS) as i:
                onehot(i, 0, False)
                add_up(i - 1, 1)
                onehot(i, 1, False)
                add_up(i, 0)
            add_up(PAIRS - 1, 1)



def norm_rows(dve, chain, m, x, out, tmp, handoff):
    known, root = handoff
    mean, v, r, y = (t[:] for t in m.stat)
    full = [P, NODE_TILES, F]
    chain(dve.tensor_reduce(mean, x, AX.X, ALU.add))
    chain(dve.tensor_scalar(mean, mean, 1.0 / F, None, ALU.mult))
    chain(dve.tensor_tensor(out, x, over(mean.unsqueeze(2), full), ALU.subtract))
    chain(dve.tensor_tensor(tmp, out, out, ALU.mult))
    chain(dve.tensor_reduce(v, tmp, AX.X, ALU.add))
    chain(dve.tensor_scalar(v, v, 1.0 / F, 1e-5, ALU.mult, ALU.add))
    chain(dve.reciprocal(r, v))
    known()
    root()
    chain(dve.tensor_tensor(r, y, y, ALU.mult))
    chain(dve.tensor_tensor(r, r, v, ALU.mult))
    chain(dve.tensor_scalar(r, r, -0.5, 1.5, ALU.mult, ALU.add))
    chain(dve.tensor_tensor(r, r, y, ALU.mult))
    chain(dve.tensor_tensor(out, out, over(r.unsqueeze(2), full), ALU.mult))


class Handoff:

    def __init__(self, dve, known, done):
        self.dve, self.known_sem, self.done_sem, self.n = dve, known, done, 0

    def known(self):
        self.dve.engine_nop().then_inc(self.known_sem, 1)
        self.n += 1

    def root(self):
        self.dve.wait_ge(self.done_sem, self.n)

    def pair(self):
        return self.known, self.root


def act_turns(block, m, known, done, turns):
    @block.scalar
    def _(act):
        for n, turn in enumerate(turns):
            act.wait_ge(known, n + 1)
            turn(act).then_inc(done, 1)


def take_root(m):
    return lambda act: act.activation(m.stat[3][:], m.stat[2][:], ACT.Sqrt)


def take_exp(view):
    return lambda act: act.activation(view, view, ACT.Exp)


def row(m, name, shape):
    return over(m.weights[name][:].unsqueeze(1), shape)


def node_product(nc, m, src, dst, w_out, hidden=None):
    C = hidden[0].shape[1] // P if hidden else 0
    cols = BLK * P
    turned_sb = m.big[:, 0:cols]
    staged = m.big[:, cols:2 * cols]
    hid = [m.big[:, (2 + c) * cols:(3 + c) * cols] for c in range(C)]
    cuts = [(lo, min(lo + 512, cols)) for lo in range(0, cols, 512)]
    ph, (staged_up, turned, copied, hid_ready, hid_done, out_ready, out_copied) = phase(
        nc, "tiles_staged", "tiles_turned", "turned_copied", "hidden_ready", "hidden_done", "out_ready", "out_copied")
    ps_turn = m.ps[0]
    ps_h0 = m.ps[1]
    ps_h1 = m.ps[2]
    ps_out = m.ps[3]
    with ph, nc.Block(no_gpsimd_drain=True) as block:
        ps_h = (ps_h0, ps_h1)

        @block.gpsimd
        def _(pool):
            def tiles(i, first):
                if not first:
                    pool.wait_ge(turned, i)
                pool.tensor_copy(staged.rearrange("p (k f) -> p k f", f=F), src[:, bass.ds(i * BLK, BLK), :]).then_inc(staged_up, 1)

            tiles(0, True)
            with pool.Fori(1, NODE_TILES // BLK) as i:
                tiles(i, False)

        @block.tensor
        def _(pe):
            def tiles(i, first):
                pe.wait_ge(staged_up, i + 1)
                for k in range(BLK):
                    t = pe.transpose(ps_turn[:, k * P:(k + 1) * P], staged[:, k * P:(k + 1) * P], m.ident[:])
                t.then_inc(turned, 1)
                pe.wait_ge(copied, i + 1)
                for c in range(C):
                    if not (first and c < 2):
                        pe.wait_ge(hid_done, i * C + (c - 1))
                    for lo, hi in cuts:
                        t = pe.matmul(ps_h[c % 2][:, lo:hi], hidden[0][:, c * P:(c + 1) * P], turned_sb[:, lo:hi], start=True, stop=True)
                    t.then_inc(hid_ready, 1)
                if C:
                    pe.wait_ge(hid_done, (i + 1) * C)
                if not first:
                    pe.wait_ge(out_copied, i)
                for k in range(BLK):
                    for c in range(max(C, 1)):
                        lhs = hid[c] if C else turned_sb
                        rhs = w_out[:, c, :] if C else w_out[:]
                        t = pe.matmul(ps_out[:, k * P:(k + 1) * P], lhs[:, k * P:(k + 1) * P], rhs, start=(c == 0), stop=(c == max(C, 1) - 1))
                t.then_inc(out_ready, 1)

            tiles(0, True)
            with pe.Fori(1, NODE_TILES // BLK) as i:
                tiles(i, False)

        @block.scalar
        def _(act):
            def tiles(i, first):
                act.wait_ge(turned, i + 1)
                if not first:
                    act.wait_ge(out_ready, i)
                act.copy(turned_sb, ps_turn[:, 0:cols]).then_inc(copied, 1)
                for c in range(C):
                    act.wait_ge(hid_ready, i * C + (c + 1))
                    act.activation(hid[c], ps_h[c % 2][:, 0:cols], hidden[2], bias=hidden[1][:, c:c + 1]).then_inc(hid_done, 1)

            tiles(0, True)
            with act.Fori(1, NODE_TILES // BLK) as i:
                tiles(i, False)

        @block.vector
        def _(dve):
            with dve.Fori(0, NODE_TILES // BLK) as i:
                dve.wait_ge(out_ready, i + 1)
                dve.tensor_copy(dst[:, bass.ds(i * BLK, BLK), :], ps_out[:, 0:cols].rearrange("p (k f) -> p k f", f=F)).then_inc(out_copied, 1)


FULL = [P, NODE_TILES, F]


def dve_phase(nc, m, turns, body):
    ph, (step, known, done) = phase(nc, "dve_step", "act_input_known", "act_done")
    with ph, nc.Block(no_gpsimd_drain=True) as block:
        act_turns(block, m, known, done, turns)

        @block.vector
        def _(dve):
            body(dve, Chain(dve, step), Handoff(dve, known, done))


def gcn(nc, m, a):
    w = m.weights
    y, mid = m.node[0], m.node[1]
    dinv = over(m.dinv[:].unsqueeze(2), FULL)

    dve_phase(nc, m, [], lambda dve, chain, hand: chain(dve.tensor_tensor(y, m.x[:], dinv, ALU.mult)))
    store_table(nc, m, 0, [(y, 0, F)])
    sum_edges(nc, m, 0)

    def scaled(dve, chain, hand):
        chain(dve.tensor_tensor(mid, m.acc[:, :, 0:F], y, ALU.add))
        chain(dve.tensor_tensor(mid, mid, dinv, ALU.mult))

    dve_phase(nc, m, [], scaled)
    node_product(nc, m, mid, y, w["L0_W2T"], (w["L0_W1T"], w["L0_b1T"], ACT.Relu))
    dve_phase(nc, m, [], lambda dve, chain, hand: chain(dve.tensor_tensor(y, y, dinv, ALU.mult)))
    store_table(nc, m, 0, [(y, 0, F)])
    sum_edges(nc, m, 0)

    def finish(dve, chain, hand):
        scaled(dve, chain, hand)
        chain(dve.tensor_tensor(mid, mid, row(m, "L0_gnn_b2", FULL), ALU.add))
        chain(dve.tensor_scalar(mid, mid, 0.0, None, ALU.max))
        chain(dve.tensor_tensor(mid, mid, m.x[:], ALU.add))
        norm_rows(dve, chain, m, mid, m.x[:], y, hand.pair())

    dve_phase(nc, m, [take_root(m)], finish)


def heads(view, H):
    return view.rearrange("p j (h c) -> p j h c", h=H)


def node_scores(nc, m, H, att_src, att_dst):
    tmp = m.node[1]

    def body(dve, chain, hand):
        xh = m.tab[:, :, 0:F]
        for name, a in ((att_src, m.a_src), (att_dst, m.a_dst)):
            chain(dve.tensor_tensor(tmp, xh, row(m, name, FULL), ALU.mult))
            chain(dve.tensor_reduce(a[:, :, 0:H], heads(tmp, H), AX.X, ALU.add))

    dve_phase(nc, m, [], body)
    store_table(nc, m, H, [(m.tab[:, :, 0:F], 0, F), (m.a_src[:, :, 0:H], F, F + H)])


def step_view(m, i, H):
    return m.big[:, i * 8 * LANES:i * 8 * LANES + H * LANES].rearrange("p (h g e) -> p h g e", h=H, e=P)


def flat(view):
    return view.rearrange("p h g e -> p h (g e)")


def spread_nodes(nc, m, H, values, raw, transpose_to=None):
    ph, (scattered, loaded, turned, copied) = phase(nc, "nodes_scattered", "spread_loaded", "lanes_turned", "turned_copied")
    ps0 = m.ps[0]
    ps1 = m.ps[1]
    with ph, nc.Block() as block:
        ps = (ps0, ps1)

        @block.gpsimd
        def _(pool):
            for j in range(NODE_TILES):
                pool.indirect_dma_start(m.d_spread[H], bass.IndirectOffsetOnAxis(ap=m.pos_first[:, j:j + 1], axis=0),
                                        values[:, j, 0:H], None).then_inc(scattered, 16)

        @block.sync
        def _(sp):
            sp.wait_ge(scattered, 16 * NODE_TILES)
            sp.dma_start(raw, m.d_spread[H][0:LANES * P, :].rearrange("(g p e) h -> p g (e h)", p=P, e=P)).then_inc(loaded, 16)
            sp.wait_ge(loaded, 16)

        if transpose_to is not None:
            @block.tensor
            def _(pe):
                for h in range(H):
                    if h >= 2:
                        pe.wait_ge(copied, h - 1)
                    for g in range(G):
                        t = pe.transpose(ps[h % 2][:, g * P:(g + 1) * P], m.lane[:, g * P:(g + 1) * P, h], m.ident[:])
                    t.then_inc(turned, 1)

            @block.scalar
            def _(act):
                for h in range(H):
                    act.wait_ge(turned, h + 1)
                    act.copy(flat(transpose_to)[:, h, :], ps[h % 2][:, 0:LANES]).then_inc(copied, 1)


class Carry:

    def __init__(self, ph, m, H):
        self.m, self.H = m, H
        self.last_known, self.rows_ready, self.scanned, self.back = (
            ph.semaphore(n) for n in ("last_lanes_known", "rows_ready", "rows_scanned", "carry_back"))
        self.ps_row, self.ps_back = m.ps[0], m.ps[1]

    def tensor(self, pe, local):
        m, H = self.m, self.H
        pe.wait_ge(self.last_known, 1)
        for g in range(G):
            t = pe.transpose(self.ps_row[0:H, g * P:(g + 1) * P], local[:, :, g, P - 1], m.ident[:])
        t.then_inc(self.rows_ready, 1)
        pe.wait_ge(self.scanned, 1)
        for g in range(G):
            t = pe.transpose(self.ps_back[:, g * 8:g * 8 + H], m.carry[0][0:H, g * P:(g + 1) * P], m.ident[0:H, 0:H])
        t.then_inc(self.back, 1)

    def vector(self, dve, chain, open_row, initial, ops):
        m, H = self.m, self.H
        dve.engine_nop().then_inc(self.last_known, 1)
        chain(dve.memset(m.carry[0][0:H, 0:1], initial))
        dve.wait_ge(self.rows_ready, 1)
        chain(dve.tensor_copy(m.carry[1][0:H, 0:LANES], self.ps_row[0:H, 0:LANES]))
        chain(dve.tensor_tensor_scan(m.carry[0][0:H, 1:LANES + 1], open_row, m.carry[1][0:H, 0:LANES], initial, *ops))
        dve.engine_nop().then_inc(self.scanned, 1)
        dve.wait_ge(self.back, 1)
        chain(dve.tensor_copy(m.step_carry[:], self.ps_back[:, 0:8 * G].rearrange("p (g h) -> p g h", h=8)))
        return over(m.step_carry[:, :, 0:H].rearrange("p g h -> p h g").unsqueeze(3), [P, H, G, P])


def fill_edges(nc, m, H, raw, out, tmp, after=None, turn=None):
    ph, (step, known, done) = phase(nc, "dve_step", "act_input_known", "act_done")
    with ph:
        carry = Carry(ph, m, H)
        with nc.Block(no_gpsimd_drain=True) as block:
            @block.tensor
            def _(pe):
                carry.tensor(pe, out)

            if turn:
                act_turns(block, m, known, done, [turn])

            @block.vector
            def _(dve):
                chain = Chain(dve, step)
                for h in range(H):
                    data = raw.rearrange("p g (e h) -> p h (g e)", h=H)[:, h, :]
                    chain(dve.tensor_tensor_scan(flat(out)[:, h, :], ge(m.keep[:]), data, 0.0, ALU.mult, ALU.add))
                before = carry.vector(dve, chain, m.open_row[0:H, :], 0.0, (ALU.mult, ALU.add))
                full = [P, H, G, P]
                chain(dve.tensor_tensor(tmp, over(m.nostart[:].unsqueeze(1), full), before, ALU.mult))
                chain(dve.tensor_tensor(out, out, tmp, ALU.add))
                if after:
                    after(dve, chain, Handoff(dve, known, done))


def leaky(dve, view):
    return dve.scalar_tensor_tensor(out=view, in0=view, scalar=0.2, in1=view, op0=ALU.mult, op1=ALU.max)


def edge_maxima(nc, m, H, alpha, local, tmp):
    ph, (step, stored, gathered, ready) = phase(nc, "dve_step", "maxima_stored", "maxima_gathered", "maxima_known")
    with ph:
        carry = Carry(ph, m, H)
        with nc.Block() as block:
            @block.tensor
            def _(pe):
                carry.tensor(pe, local)

            @block.sync
            def _(sp):
                sp.wait_ge(ready, 1)
                sp.dma_start(m.d_max[H].rearrange("(g p e) h -> p g (e h)", p=P, e=P),
                             tmp.rearrange("p h g e -> p (h g e)").rearrange("p (g r) -> p g r", g=G)).then_inc(stored, 16)

            @block.gpsimd
            def _(pool):
                pool.wait_ge(stored, 16)
                for j in range(NODE_TILES):
                    pool.indirect_dma_start(m.node_m[:, j, 0:H], None, m.d_max[H],
                                            bass.IndirectOffsetOnAxis(ap=m.pos_last[:, j:j + 1], axis=0)).then_inc(gathered, 16)
                pool.wait_ge(gathered, 16 * NODE_TILES)

            @block.vector
            def _(dve):
                chain = Chain(dve, step)
                pen = m.acc[:].rearrange("p j f -> p (j f)")[:, 0:LANES]
                open_pen = m.acc[0:H].rearrange("p j f -> p (j f)")[:, LANES:2 * LANES]
                chain(dve.tensor_scalar(pen, ge(m.keep[:]), -1.0, -NEG, ALU.add, ALU.mult))
                chain(dve.tensor_scalar(open_pen, m.open_row[0:H, :], -1.0, -NEG, ALU.add, ALU.mult))
                for h in range(H):
                    chain(dve.tensor_tensor_scan(flat(local)[:, h, :], pen, flat(alpha)[:, h, :], NEG, ALU.add, ALU.max))
                before = carry.vector(dve, chain, open_pen, NEG, (ALU.add, ALU.max))
                full = [P, H, G, P]
                chain(dve.tensor_scalar(pen, ge(m.nostart[:]), -1.0, -NEG, ALU.add, ALU.mult))
                pen4 = over(pen.rearrange("p (g e) -> p g e", e=P).unsqueeze(1), full)
                chain(dve.tensor_tensor(tmp, pen4, before, ALU.add))
                chain(dve.tensor_tensor(local, local, tmp, ALU.max))
                by_lane = tmp.rearrange("p h g e -> p (h g e)").rearrange("p (r h) -> p r h", h=H)
                chain(dve.tensor_copy(by_lane, flat(local).rearrange("p h r -> p r h")))
                dve.engine_nop().then_inc(ready, 1)


def turn_back(nc, m, H, coef):
    ph, (turned, copied) = phase(nc, "coefs_turned", "coefs_copied")
    ps0 = m.ps[0]
    ps1 = m.ps[1]
    with ph, nc.Block(no_gpsimd_drain=True) as block:
        ps = (ps0, ps1)

        @block.tensor
        def _(pe):
            for h in range(H):
                if h >= 2:
                    pe.wait_ge(copied, h - 1)
                for g in range(G):
                    t = pe.transpose(ps[h % 2][:, g * P:(g + 1) * P], coef[:, h, g, :], m.ident[:])
                t.then_inc(turned, 1)

        @block.scalar
        def _(act):
            for h in range(H):
                act.wait_ge(turned, h + 1)
                act.copy(m.lane[:, :, h], ps[h % 2][:, 0:LANES]).then_inc(copied, 1)


def attention(nc, m, H, att_src, att_dst, self_loops, a):
    node_scores(nc, m, H, att_src, att_dst)
    gather_rows(nc, m, H)
    alpha, work, spread = (step_view(m, i, H) for i in range(3))

    def as_raw(view):
        return view.rearrange("p h g e -> p (h g e)").rearrange("p (g r) -> p g r", g=G)

    spread_nodes(nc, m, H, m.a_dst, as_raw(work), transpose_to=alpha)
    full = [P, H, G, P]
    sa, nm = m.self_a[:, :, 0:H], m.node_m[:, :, 0:H]
    if not self_loops:
        edge_weights(nc, m, a)

    def scores(dve, chain, hand):
        chain(dve.tensor_tensor(alpha, alpha, spread, ALU.add))
        if not self_loops:
            weights = m.tab_weights
            chain(dve.tensor_tensor(alpha, alpha, over(weights.unsqueeze(1), full), ALU.mult))
        chain(leaky(dve, flat(alpha)))
        chain(dve.tensor_tensor(alpha, alpha, over(m.valid[:].unsqueeze(1), full), ALU.mult))
        neg = m.acc[:].rearrange("p j f -> p (j f)")[:, 0:LANES]
        chain(dve.tensor_scalar(neg, ge(m.valid[:]), -1.0, -NEG, ALU.add, ALU.mult))
        chain(dve.tensor_tensor(alpha, alpha, over(neg.rearrange("p (g e) -> p g e", e=P).unsqueeze(1), full), ALU.add))
        if self_loops:
            chain(dve.tensor_tensor(sa, m.a_src[:, :, 0:H], m.a_dst[:, :, 0:H], ALU.add))
            chain(leaky(dve, sa))

    fill_edges(nc, m, H, as_raw(work), spread, work, scores)
    edge_maxima(nc, m, H, alpha, work, spread)

    def node_max(dve, chain, hand):
        has = over(m.has[:].unsqueeze(2), [P, NODE_TILES, H])
        chain(dve.tensor_tensor(nm, nm, has, ALU.mult))
        if self_loops:
            t = m.stat[0][:]
            chain(dve.tensor_scalar(t, m.has[:], -1.0, -NEG, ALU.add, ALU.mult))
            chain(dve.tensor_tensor(nm, nm, over(t.unsqueeze(2), [P, NODE_TILES, H]), ALU.add))
            chain(dve.tensor_tensor(nm, nm, sa, ALU.max))
            chain(dve.tensor_tensor(sa, sa, nm, ALU.subtract))
            hand.known()
            hand.root()

    dve_phase(nc, m, [take_exp(sa)] if self_loops else [], node_max)
    spread_nodes(nc, m, H, m.node_m, as_raw(work))

    def exps(dve, chain, hand):
        chain(dve.tensor_tensor(alpha, alpha, spread, ALU.subtract))
        hand.known()
        hand.root()

    fill_edges(nc, m, H, as_raw(work), spread, work, exps, take_exp(alpha.rearrange("p h g e -> p (h g e)")))
    turn_back(nc, m, H, alpha)
    sum_edges(nc, m, H)


def edge_weights(nc, m, a):
    m.tab_weights = m.acc[:].rearrange("p j f -> p (j f)")[:, LANES:2 * LANES].rearrange("p (g e) -> p g e", e=P)
    ph, (gathered,) = phase(nc, "weights_gathered")
    with ph, nc.Block() as block:
        @block.gpsimd
        def _(pool):
            for g in range(G):
                pool.indirect_dma_start(m.tab_weights[:, g, :], None, a["edge_weight"],
                                        bass.IndirectOffsetOnAxis(ap=m.step_tile[:, g:g + 1], axis=0)).then_inc(gathered, 16)
            pool.wait_ge(gathered, 16 * G)


def finish_sums(dve, chain, m, H, out, self_loops, eps):
    den = m.acc[:, :, F:F + H]
    shape = [P, NODE_TILES, H]
    c = F // H
    if self_loops:
        wide = over(m.self_a[:, :, 0:H].unsqueeze(3), [P, NODE_TILES, H, c])
        chain(dve.tensor_tensor(heads(out, H), heads(m.tab[:, :, 0:F], H), wide, ALU.mult))
        chain(dve.tensor_tensor(out, out, m.acc[:, :, 0:F], ALU.add))
        chain(dve.tensor_tensor(den, den, m.self_a[:, :, 0:H], ALU.add))
    if eps:
        chain(dve.tensor_scalar(den, den, eps, None, ALU.add))
    chain(dve.reciprocal(m.node_m[:, :, 0:H], den))
    wide = over(m.node_m[:, :, 0:H].unsqueeze(3), [P, NODE_TILES, H, c])
    src = out if self_loops else m.acc[:, :, 0:F]
    chain(dve.tensor_tensor(heads(out, H), heads(src, H), wide, ALU.mult))


def gat(nc, m, a):
    w = m.weights
    node_product(nc, m, m.x, m.tab[:, :, 0:F], w["L1_gnn_W"])
    attention(nc, m, 4, "L1_gnn_att_src", "L1_gnn_att_dst", True, a)
    o, t, u = m.node

    def finish(dve, chain, hand):
        finish_sums(dve, chain, m, 4, o, True, 1e-16)
        chain(dve.tensor_tensor(o, o, row(m, "L1_gnn_bias", FULL), ALU.add))
        norm_rows(dve, chain, m, o, t, u, hand.pair())
        chain(dve.tensor_tensor(t, t, row(m, "L1_gnn_ln_w", FULL), ALU.mult))
        chain(dve.tensor_tensor(t, t, row(m, "L1_gnn_ln_b", FULL), ALU.add))
        chain(dve.tensor_scalar(u, t, 0.0, w["L1_gnn_prelu_w"][:, 0:1], ALU.min, ALU.mult))
        chain(dve.tensor_scalar(t, t, 0.0, None, ALU.max))
        chain(dve.tensor_tensor(t, t, u, ALU.add))
        chain(dve.tensor_tensor(t, t, m.x[:], ALU.add))
        norm_rows(dve, chain, m, t, m.x[:], u, hand.pair())

    dve_phase(nc, m, [take_root(m)] * 2, finish)


def weighted_gat(nc, m, a):
    w = m.weights
    node_product(nc, m, m.x, m.tab[:, :, 0:F], w["L2_gnn_W"])
    attention(nc, m, 8, "L2_gnn_att_l", "L2_gnn_att_r", False, a)
    o, t, u = m.node
    node_product(nc, m, m.x, u, w["L2_gnn_W_res"])

    def finish(dve, chain, hand):
        finish_sums(dve, chain, m, 8, o, False, 1e-16)
        chain(dve.tensor_scalar(t, o, 0.0, None, ALU.min))
        hand.known()
        chain(dve.tensor_scalar(o, o, 0.0, -1.0, ALU.max, ALU.add))
        hand.root()
        chain(dve.tensor_tensor(o, o, t, ALU.add))
        chain(dve.tensor_tensor(o, o, u, ALU.add))
        chain(dve.tensor_tensor(o, o, m.x[:], ALU.add))
        norm_rows(dve, chain, m, o, m.x[:], t, hand.pair())

    dve_phase(nc, m, [take_exp(t), take_root(m)], finish)


def transformer_gat(nc, m, a):
    w = m.weights
    o, t, u = m.node

    def before(dve, chain, hand):
        norm_rows(dve, chain, m, m.x[:], t, u, hand.pair())
        chain(dve.tensor_tensor(t, t, row(m, "L3_gnn_ln1_g", FULL), ALU.mult))
        chain(dve.tensor_tensor(t, t, row(m, "L3_gnn_ln1_b", FULL), ALU.add))

    dve_phase(nc, m, [take_root(m)], before)
    node_product(nc, m, t, m.tab[:, :, 0:F], w["L3_gnn_W"])
    attention(nc, m, 4, "L3_gnn_att_src", "L3_gnn_att_dst", True, a)

    def middle(dve, chain, hand):
        finish_sums(dve, chain, m, 4, o, True, 0.0)
        chain(dve.tensor_tensor(o, o, row(m, "L3_gnn_gat_b", FULL), ALU.add))
        chain(dve.tensor_tensor(o, o, m.x[:], ALU.add))
        norm_rows(dve, chain, m, o, t, u, hand.pair())
        chain(dve.tensor_tensor(t, t, row(m, "L3_gnn_ln2_g", FULL), ALU.mult))
        chain(dve.tensor_tensor(t, t, row(m, "L3_gnn_ln2_b", FULL), ALU.add))

    dve_phase(nc, m, [take_root(m)], middle)
    node_product(nc, m, t, u, w["L3_gnn_w2"], (w["L3_gnn_w1"], w["L3_b1T"], ACT.Gelu))

    def finish(dve, chain, hand):
        chain(dve.tensor_tensor(u, u, row(m, "L3_gnn_b2", FULL), ALU.add))
        chain(dve.tensor_tensor(u, u, o, ALU.add))
        chain(dve.tensor_tensor(u, u, m.x[:], ALU.add))
        norm_rows(dve, chain, m, u, m.x[:], t, hand.pair())

    dve_phase(nc, m, [take_root(m)], finish)


def store_output(nc, m, out):
    full = N // P
    ph, (stored,) = phase(nc, "output_stored")
    with ph, nc.Block() as block:
        @block.sync
        def _(sp):
            sp.dma_start(out[0:full * P, :].rearrange("(j p) f -> p j f", p=P), m.x[:, 0:full, :]).then_inc(stored, 16)
            sp.dma_start(out[full * P:N, :], m.x[0:N - full * P, full, :]).then_inc(stored, 16)
            sp.wait_ge(stored, 32)


def program(nc, a, out, upto=99, dump=None):
    Phase.used, Phase.count = [], 0
    with ExitStack() as ctx:
        m = Net()
        allocate(nc, ctx, m)
        load_parameters(nc, ctx, m, a)
        step_tables(nc, m, a)
        if upto >= 1:
            step_edges(nc, m, a)
            row_pointers(nc, m, a)
        end_of_layer(nc)
        for n, layer in enumerate((gcn, gat, weighted_gat, transformer_gat)):
            if upto >= n + 2:
                layer(nc, m, a)
                end_of_layer(nc)
        if dump: dump(nc, m)
        store_output(nc, m, out)


def layout(inputs):
    import numpy as np
    v = {k: np.asarray(x) for k, x in inputs.items()}
    a = {"x": np.zeros((NPAD, F), np.float32)}
    a["x"][:N] = v["x"]

    def edges(x, fill):
        padded = np.full(EPAD, fill, x.dtype)
        padded[:E] = x
        return padded

    dst = edges(v["dst"], NPAD - 1)
    a["dst"] = dst.reshape(EDGE_TILES, P)
    a["dst_before"] = np.concatenate([np.full(1, -1, dst.dtype), dst[:-1]]).reshape(EDGE_TILES, P)
    a["tile_last"] = np.ascontiguousarray(a["dst"][:, -1]).reshape(1, EDGE_TILES)
    a["src"] = edges(v["src"], 0).reshape(EDGE_TILES, P)
    a["edge_weight"] = edges(v["edge_weight"], 0).reshape(EDGE_TILES, P)
    for n in ("L0_gnn_b2", "L1_gnn_att_src", "L1_gnn_att_dst", "L1_gnn_bias", "L1_gnn_ln_w", "L1_gnn_ln_b",
              "L1_gnn_prelu_w", "L2_gnn_att_l", "L2_gnn_att_r", "L3_gnn_ln1_g", "L3_gnn_ln1_b", "L3_gnn_att_src",
              "L3_gnn_att_dst", "L3_gnn_gat_b", "L3_gnn_ln2_g", "L3_gnn_ln2_b", "L3_gnn_b2"):
        a[n] = v[n].reshape(1, -1)
    for n in ("L1_gnn_W", "L2_gnn_W", "L2_gnn_W_res", "L3_gnn_W", "L3_gnn_w1", "L3_gnn_w2"):
        a[n] = v[n]
    a["L0_W1T"] = v["L0_gnn_W1"].T
    a["L0_W2T"] = v["L0_gnn_W2"].T
    a["L0_b1T"] = v["L0_gnn_b1"].reshape(-1, P).T
    a["L3_b1T"] = v["L3_gnn_b1"].reshape(-1, P).T
    return {k: np.ascontiguousarray(x) for k, x in a.items()}


def kernel(**inputs):
    import concourse.bacc as bacc
    from concourse.bass_utils import run_bass_kernel_spmd

    nc = bacc.Bacc("TRN2", target_bir_lowering=False, num_devices=1)
    arrays = {"in_" + k: x for k, x in layout(inputs).items()}
    a = {k[3:]: nc.dram_tensor(k, x.shape, mybir.dt.from_np(x.dtype), kind="ExternalInput").ap() for k, x in arrays.items()}
    out = nc.dram_tensor("out", (N, F), F32, kind="ExternalOutput").ap()
    program(nc, a, out)
    return run_bass_kernel_spmd(nc, [arrays], core_ids=[0]).results[0]["out"]
```

```python
from contextlib import ExitStack

import concourse.bass as bass
from concourse import mybir

F32 = mybir.dt.float32
I32 = mybir.dt.int32
ALU = mybir.AluOpType
ACT = mybir.ActivationFunctionType
AX = mybir.AxisListType

P = 128
N = 3125
E = 100000
F = 128
NODE_TILES = -(-N // P)
NPAD = NODE_TILES * P
EDGE_TILES = -(-E // P)
EPAD = EDGE_TILES * P
UNIT_TILES = EDGE_TILES // 2
REAL_STEPS = 2 * (UNIT_TILES + NODE_TILES - 1)
U = 16
UNITS = U // 2
PAIRS = -(-REAL_STEPS // (2 * U))
STEPS = PAIRS * 2 * U
G = -(-STEPS // P)
LANES = G * P
NEG = -1.0e30
PER_BANK = 3
BANKS = -(-UNITS // PER_BANK)
ACT_HOTS = 4
BLK = 5
assert NODE_TILES % BLK == 0 and EDGE_TILES % 2 == 0 and STEPS <= LANES and 2 * BANKS <= 8


class Chain:

    def __init__(self, eng, sem):
        self.eng, self.sem, self.n = eng, sem, 0

    def __call__(self, ins):
        self.n += 1
        ins.then_inc(self.sem, 1)
        self.eng.wait_ge(self.sem, self.n)


def over(ap, shape):
    return ap.to_broadcast(shape)


class Net:
    pass


class Phase:

    used = []
    count = 0

    def __init__(self, nc):
        self.nc = nc

    def __enter__(self):
        return self

    def __exit__(self, *error):
        return False

    def semaphore(self, name):
        sem = self.nc.alloc_semaphore(f"{name}_{Phase.count}")
        Phase.used.append(sem)
        Phase.count += 1
        return sem


def phase(nc, *names):
    ph = Phase(nc)
    return ph, [ph.semaphore(n) for n in names]


def end_of_layer(nc):
    nc.all_engine_barrier()
    nc.clear_and_free_semaphores(Phase.used)
    Phase.used = []
    nc.all_engine_barrier()


def allocate(nc, ctx, m):
    def sb(name, shape, dt=F32):
        return ctx.enter_context(nc.sbuf_tensor(name, shape, dt))

    m.iota = sb("iota_row", [P, P])
    m.ident = sb("identity", [P, P])
    m.x = sb("node_x", [P, NODE_TILES, F])
    m.tab = sb("node_table", [P, NODE_TILES, F + 8])
    m.acc = sb("node_sums", [P, NODE_TILES, F + 8])
    m.drel = sb("lane_dst_rel", [P, LANES])
    m.src = sb("lane_src", [P, LANES], I32)
    m.jrow = sb("unit_node_tile", [1, LANES // 2], I32)
    m.keep = sb("step_keep", [P, G, P])
    m.cap = sb("step_cap", [P, G, P])
    m.end = sb("step_end", [P, G, P])
    m.noend = sb("step_noend", [P, G, P])
    m.nostart = sb("step_nostart", [P, G, P])
    m.lane = sb("lane_coef", [P, LANES, 8])
    m.big = sb("work", [P, 3 * 8 * LANES])
    m.carry = [sb(f"carry{i}", [8, LANES + 1]) for i in range(2)]
    m.dinv = sb("node_dinv", [P, NODE_TILES])
    m.has = sb("node_has_edges", [P, NODE_TILES])
    m.pos_first = sb("node_pos_first", [P, NODE_TILES], I32)
    m.a_src = sb("node_a_src", [P, NODE_TILES, 8])
    m.spread = sb("node_spread", [P, NODE_TILES, 8])
    m.self_p = sb("node_self_weight", [P, NODE_TILES, 8])
    m.inv = sb("node_reciprocal", [P, NODE_TILES, 8])
    m.stat = [sb(f"node_stat{i}", [P, NODE_TILES]) for i in range(4)]
    m.node_no = sb("node_number", [P, NODE_TILES])
    m.step_no = sb("step_number", [P, G], I32)
    m.step_tile = sb("step_edge_tile", [P, G], I32)
    m.step_base = sb("step_node_base", [P, G])
    m.open_row = sb("row_nostart", [8, LANES])
    m.open_back = sb("row_noend", [8, LANES])
    m.step_carry = sb("step_carry", [P, G, 8])
    m.idx_row = sb("step_j_rows", [8, P], I32)
    m.j_regs = [nc.vector.alloc_register(f"unit_j{k}") for k in range(UNITS)]
    m.weights = {}
    R = U * (F + 8)
    big = m.big
    m.ring = [big[:, h * R:(h + 1) * R] for h in range(2)]
    m.msg = [big[:, (2 + h) * R:(3 + h) * R] for h in range(2)]
    m.onehot = [big[:, 4 * R + h * U * P:4 * R + (h + 1) * U * P].rearrange("p (u d) -> p u d", d=P) for h in range(2)]
    base = 4 * R + 2 * U * P
    m.idx = [sb(f"gather_index{h}", [P, U], I32) for h in range(2)]
    W = NODE_TILES * F
    m.node = [big[:, lo:lo + W].rearrange("p (j f) -> p j f", f=F) for lo in (base, base + W, 6 * BLK * P)]
    m.acc_odd = big[:, base + W:base + W + NODE_TILES * (F + 8)].rearrange("p (j f) -> p j f", f=F + 8)
    free = m.acc[:].rearrange("p j f -> p (j f)")
    m.edge_w = free[:, 0:LANES].rearrange("p (g e) -> p g e", e=P)
    m.pen = free[:, LANES:2 * LANES]
    m.open_pen = free[:, 2 * LANES:3 * LANES]
    assert base + 2 * W <= 3 * 8 * LANES and 6 * BLK * P + W <= base
    assert base + W + NODE_TILES * (F + 8) <= 3 * 8 * LANES

    m.ps = [ctx.enter_context(nc.psum_tensor(f"psum{i}", [P, 1024], F32)) for i in range(4)]

    def dram(name, shape, dt=F32):
        return nc.dram_tensor(name, shape, dt, kind="Internal").ap()

    m.d_table = {H: dram(f"table_{H}", [NPAD, F + H]) for H in (0, 4, 8)}
    m.d_rows = {H: dram(f"rows_{H}", [P, STEPS, F + H]) for H in (4, 8)}
    m.d_spread = dram("spread", [LANES * P + NPAD, 8])
    m.d_j = dram("unit_j", [G, P // 2], I32)
    m.d_ptr = dram("row_ptr", [NPAD + 1, 1])


WEIGHTS = (
    (("L0_gnn_b2",), ("L0_W1T", "L0_b1T"), ("L0_W2T",)),
    (("L1_gnn_att_src", "L1_gnn_att_dst", "L1_gnn_bias", "L1_gnn_ln_w", "L1_gnn_ln_b", "L1_gnn_prelu_w"), ("L1_gnn_W",), ()),
    (("L2_gnn_att_l", "L2_gnn_att_r"), ("L2_gnn_W", "L2_gnn_W_res"), ()),
    (("L3_gnn_ln1_g", "L3_gnn_ln1_b", "L3_gnn_att_src", "L3_gnn_att_dst", "L3_gnn_gat_b", "L3_gnn_ln2_g", "L3_gnn_ln2_b",
      "L3_gnn_b2"), ("L3_gnn_W", "L3_gnn_w1", "L3_b1T"), ("L3_gnn_w2",)))


def load_weights(nc, ctx, m, a, layer):
    vectors, plain, chunked = WEIGHTS[layer]
    w = m.weights
    for n in vectors + plain:
        w[n] = ctx.enter_context(nc.sbuf_tensor("w_" + n, [P, a[n].shape[1]], F32))
    for n in chunked:
        w[n] = ctx.enter_context(nc.sbuf_tensor("w_" + n, [P, a[n].shape[0] // P, F], F32))
    ph, (loaded,) = phase(nc, "weights_loaded")
    with ph, nc.Block(no_gpsimd_drain=True) as block:
        @block.sync
        def _(sp):
            for n in vectors:
                sp.dma_start(w[n][:], over(a[n], [P, a[n].shape[1]])).then_inc(loaded, 16)
            for n in plain:
                sp.dma_start(w[n][:], a[n]).then_inc(loaded, 16)
            for n in chunked:
                sp.dma_start(w[n][:], a[n].rearrange("(c p) f -> p c f", p=P)).then_inc(loaded, 16)
            sp.wait_ge(loaded, 16 * len(vectors + plain + chunked))


def load_parameters(nc, m, a):
    ph, (loaded, iota_done, zeroed) = phase(nc, "params_loaded", "iota_done", "zeroed")
    with ph, nc.Block() as block:
        @block.sync
        def _(sp):
            sp.dma_start(m.x[:], a["x"].rearrange("(j p) f -> p j f", p=P)).then_inc(loaded, 16)
            sp.wait_ge(zeroed, 1)
            sp.dma_start(m.d_spread[0:LANES * P, :].rearrange("(p r) h -> p (r h)", p=P),
                         m.big[:, 0:LANES * 8]).then_inc(loaded, 16)
            sp.wait_ge(loaded, 32)

        @block.gpsimd
        def _(pool):
            chain = Chain(pool, iota_done)
            chain(pool.iota(m.iota[:], [[1, P]], base=0, channel_multiplier=0, allow_small_or_imprecise_dtypes=True))
            chain(pool.iota(m.node_no[:], [[P, NODE_TILES]], base=0, channel_multiplier=1, allow_small_or_imprecise_dtypes=True))
            chain(pool.iota(m.step_no[:], [[P, G]], base=0, channel_multiplier=1))
            chain(pool.iota(m.carry[0][0:1, 0:EDGE_TILES], [[1, EDGE_TILES]], base=1, channel_multiplier=0,
                            allow_small_or_imprecise_dtypes=True))
            chain(pool.memset(m.ident[:], 0.0))
            chain(pool.affine_select(out=m.ident[:], in_=m.ident[:], compare_op=ALU.not_equal, fill=1.0,
                                     base=0, pattern=[[-1, P]], channel_multiplier=1))

        @block.vector
        def _(dve):
            dve.memset(m.big[:, 0:8 * LANES], 0.0).then_inc(zeroed, 1)
            dve.memset(m.lane[:], 0.0)


def ge(ap):
    return ap.rearrange("p g e -> p (g e)")


def step_tables(nc, m, a):
    T, T2 = EDGE_TILES, UNIT_TILES
    rows = [m.big[:, i * T:(i + 1) * T] for i in range(6)]
    last_i, last_f, begin, begin_all, hit, spare = rows
    at = 6 * T
    unit, odd, t_of, j_of, j_cap, unit_i, odd_i = (m.big[:, at + i * G:at + (i + 1) * G] for i in range(7))
    at += 7 * G
    ones = m.big[:, at:at + P]
    m.last_all = m.tab[:].rearrange("p j f -> p (j f)")[:, 0:T]
    ph, (loaded, dve_step, spread, tiles_known, turned, stored) = phase(
        nc, "loaded", "dve_step", "rows_spread", "tiles_known", "j_turned", "j_stored")
    ps_begin = m.ps[0]
    ps_last = m.ps[1]
    ps_j = m.ps[2]
    with ph, nc.Block() as block:

        @block.sync
        def _(sp):
            sp.dma_start(last_i[0:1, :].bitcast(I32), a["tile_last"]).then_inc(loaded, 16)
            sp.wait_ge(tiles_known, 2)
            sp.dma_start(m.d_j, m.idx_row[0:G, 0:P // 2]).then_inc(stored, 16)
            sp.wait_ge(stored, 16)
            sp.dma_start(m.jrow[:], m.d_j.rearrange("(a g) p -> a (g p)", a=1)).then_inc(stored, 16)
            sp.wait_ge(stored, 32)

        @block.tensor
        def _(pe):
            pe.wait_ge(dve_step, 5)
            for row, out, n in ((begin, ps_begin, T2), (last_f, ps_last, T)):
                for lo in range(0, n, 512):
                    hi = min(lo + 512, n)
                    pe.matmul(out[:, lo:hi], ones[0:1, :], row[0:1, lo:hi], start=True, stop=True).then_inc(spread, 1)
            pe.wait_ge(tiles_known, 1)
            pe.transpose(ps_j[0:G, 0:P], j_cap, m.ident[:]).then_inc(turned, 1)

        @block.vector
        def _(dve):
            chain = Chain(dve, dve_step)
            chain(dve.memset(ones, 1.0))
            dve.wait_ge(loaded, 16)
            chain(dve.tensor_scalar(spare[0:1, :].bitcast(I32), last_i[0:1, :].bitcast(I32), 7, None, ALU.logical_shift_right))
            chain(dve.tensor_copy(hit[0:1, :], spare[0:1, :].bitcast(I32)))
            chain(dve.tensor_copy(last_f[0:1, :], last_i[0:1, :].bitcast(I32)))
            chain(dve.tensor_tensor(begin[0:1, 0:T2], hit[0:1, 1:T:2], m.carry[0][0:1, 0:T2], ALU.add))
            chain(dve.tensor_scalar(unit_i.bitcast(I32), m.step_no[:], 1, None, ALU.logical_shift_right))
            chain(dve.tensor_scalar(odd_i.bitcast(I32), m.step_no[:], 1, None, ALU.bitwise_and))
            chain(dve.tensor_copy(unit, unit_i.bitcast(I32)))
            chain(dve.tensor_copy(odd, odd_i.bitcast(I32)))
            dve.wait_ge(spread, 3)
            chain(dve.tensor_copy(begin_all[:, 0:T2], ps_begin[:, 0:T2]))
            chain(dve.tensor_copy(m.last_all, ps_last[:, 0:T]))
            for g in range(G):
                chain(dve.tensor_scalar(hit[:, 0:T2 - 1], begin_all[:, 0:T2 - 1], unit[:, g:g + 1], None, ALU.is_le))
                chain(dve.tensor_reduce(t_of[:, g:g + 1], hit[:, 0:T2 - 1], AX.X, ALU.add))
            chain(dve.tensor_tensor(j_of, unit, t_of, ALU.subtract))
            chain(dve.scalar_tensor_tensor(out=unit, in0=t_of, scalar=2.0, in1=odd, op0=ALU.mult, op1=ALU.add))
            chain(dve.tensor_copy(m.step_tile[:], unit))
            chain(dve.tensor_scalar(m.step_base[:], j_of, float(P), None, ALU.mult))
            chain(dve.tensor_scalar(j_cap, j_of, float(NODE_TILES - 1), None, ALU.min))
            dve.engine_nop().then_inc(tiles_known, 1)
            dve.wait_ge(turned, 1)
            dve.tensor_copy(m.idx_row[0:G, 0:P // 2], ps_j[0:G, 0:P:2]).then_inc(tiles_known, 1)


def pointer_buffers(m):
    T, JP, at = EDGE_TILES, NODE_TILES * P, 12 * LANES
    rows_i = m.big[:, at:at + JP].bitcast(I32).rearrange("p (j e) -> p j e", e=P)
    hit = m.big[:, at + JP:at + JP + T]
    tiles_before = m.big[:, at + JP + T:at + JP + T + NODE_TILES]
    assert at + JP + T + NODE_TILES <= 3 * 8 * LANES
    return rows_i, hit, tiles_before


def step_edges(nc, m, a):
    rows_i, hit, tiles_before = pointer_buffers(m)
    tiles_int = m.pos_first
    def part(i):
        return m.big[:, i * LANES:(i + 1) * LANES].rearrange("p (g e) -> p g e", e=P)

    names = ("dst", "dst_before", "dst_after", "src")
    raw = {n: part(i).bitcast(I32) for i, n in enumerate(names)}
    dst, before, after, src, start, rel, valid, tmp = (part(4 + i) for i in range(8))
    ph, (gathered, dve_step, rel_known, open_known, turned, tiles_known, rows_in) = phase(
        nc, "edges_gathered", "dve_step", "rel_known", "open_known", "edges_turned", "tiles_known", "rows_gathered")
    ps_rel, ps_src, ps_open, ps_open_back = m.ps
    with ph, nc.Block() as block:

        @block.gpsimd
        def _(pool):
            for n in names:
                for g in range(G):
                    pool.indirect_dma_start(raw[n][:, g, :], None, a[n],
                                            bass.IndirectOffsetOnAxis(ap=m.step_tile[:, g:g + 1], axis=0)).then_inc(gathered, 16)
            pool.wait_ge(tiles_known, 1)
            for j in range(NODE_TILES):
                pool.indirect_dma_start(rows_i[:, j, :], None, a["dst"],
                                        bass.IndirectOffsetOnAxis(ap=tiles_int[:, j:j + 1], axis=0)).then_inc(rows_in, 16)
            pool.wait_ge(rows_in, 16 * NODE_TILES)

        @block.tensor
        def _(pe):
            pe.wait_ge(rel_known, 1)
            for g in range(G):
                pe.transpose(ps_rel[:, g * P:(g + 1) * P], rel[:, g, :], m.ident[:]).then_inc(turned, 1)
                pe.transpose(ps_src[:, g * P:(g + 1) * P], src[:, g, :], m.ident[:]).then_inc(turned, 1)
            for n, out in enumerate((ps_open, ps_open_back)):
                pe.wait_ge(open_known, n + 1)
                for g in range(G):
                    pe.transpose(out[0:8, g * P:(g + 1) * P], m.step_carry[:, g, :], m.ident[:]).then_inc(turned, 1)

        @block.vector
        def _(dve):
            chain = Chain(dve, dve_step)
            for j in range(NODE_TILES):
                chain(dve.tensor_scalar(hit, m.last_all, m.node_no[:, j:j + 1], None, ALU.is_lt))
                chain(dve.tensor_reduce(tiles_before[:, j:j + 1], hit, AX.X, ALU.add))
            dve.tensor_copy(tiles_int[:], tiles_before).then_inc(tiles_known, 1)
            dve.wait_ge(gathered, 16 * len(names) * G)
            for n, out in zip(names, (dst, before, after, src)):
                chain(dve.tensor_copy(out, raw[n]))
            chain(dve.tensor_tensor(rel, dst, over(m.step_base[:].unsqueeze(2), [P, G, P]), ALU.subtract))
            dve.engine_nop().then_inc(rel_known, 1)
            chain(dve.tensor_scalar(valid, rel, 0.0, None, ALU.is_ge))
            chain(dve.tensor_scalar(tmp, rel, float(P), None, ALU.is_lt))
            chain(dve.tensor_tensor(valid, valid, tmp, ALU.mult))
            chain(dve.tensor_scalar(m.cap[:], valid, -0.5, -2.0 * NEG, ALU.add, ALU.mult))
            chain(dve.tensor_tensor(start, dst, before, ALU.not_equal))
            chain(dve.tensor_tensor(start, start, valid, ALU.mult))
            chain(dve.tensor_tensor(tmp, dst, after, ALU.not_equal))
            chain(dve.tensor_tensor(m.end[:], tmp, valid, ALU.mult))
            chain(dve.tensor_scalar(m.keep[:], start, -1.0, 1.0, ALU.mult, ALU.add))
            chain(dve.memset(m.keep[:, :, 0:1], 0.0))
            chain(dve.tensor_tensor_scan(ge(before), ge(m.keep[:]), ge(start), 0.0, ALU.mult, ALU.add))
            chain(dve.tensor_scalar(m.nostart[:], before, -1.0, 1.0, ALU.mult, ALU.add))
            chain(dve.tensor_copy(m.step_carry[:], over(m.nostart[:, :, P - 1:P], [P, G, 8])))
            dve.engine_nop().then_inc(open_known, 1)
            chain(dve.tensor_scalar(tmp, m.end[:], -1.0, 1.0, ALU.mult, ALU.add))
            chain(dve.memset(tmp[:, :, P - 1:P], 0.0))
            chain(dve.tensor_tensor_scan(ge(after)[:, ::-1], ge(tmp)[:, ::-1], ge(m.end[:])[:, ::-1], 0.0,
                                         ALU.mult, ALU.add))
            chain(dve.tensor_scalar(m.noend[:], after, -1.0, 1.0, ALU.mult, ALU.add))
            dve.wait_ge(turned, 3 * G)
            chain(dve.tensor_copy(m.step_carry[:], over(m.noend[:, :, 0:1], [P, G, 8])))
            dve.engine_nop().then_inc(open_known, 1)
            chain(dve.tensor_copy(m.drel[:], ps_rel[:, 0:LANES]))
            chain(dve.tensor_copy(m.src[:], ps_src[:, 0:LANES]))
            chain(dve.tensor_copy(m.open_row[:], ps_open[0:8, 0:LANES]))
            dve.wait_ge(turned, 4 * G)
            chain(dve.tensor_copy(m.open_back[:], ps_open_back[0:8, 0:LANES]))


def row_pointers(nc, m, a):
    JP = NODE_TILES * P
    rows_i, _, tiles_before = pointer_buffers(m)
    rows = m.big[:, 0:JP].rearrange("p (j e) -> p j e", e=P)
    at = JP
    in_tile, ptr, ptr_next, s0, s1, s2 = (m.big[:, at + i * NODE_TILES:at + (i + 1) * NODE_TILES] for i in range(6))
    at += 6 * NODE_TILES
    ptr_row, next_row, last = (m.big[:, at + i * P:at + (i + 1) * P] for i in range(3))
    ph, (dve_step, ptr_known, turned, row_known, stored, loaded, deg_known, root) = phase(
        nc, "dve_step", "ptr_known", "ptr_turned", "row_known", "ptr_stored",
        "next_loaded", "degree_known", "root_done")
    ps_row = m.ps[0]
    ps_next = m.ps[1]
    with ph, nc.Block() as block:

        @block.sync
        def _(sp):
            sp.wait_ge(row_known, 1)
            sp.dma_start(m.d_ptr[0:NPAD, :].rearrange("(j p) a -> j (p a)", p=P), ptr_row[0:NODE_TILES, :]).then_inc(stored, 16)
            sp.dma_start(m.d_ptr[NPAD:NPAD + 1, :], last[0:1, 0:1]).then_inc(stored, 16)
            sp.wait_ge(stored, 32)
            sp.dma_start(next_row[0:NODE_TILES, :], m.d_ptr[1:NPAD + 1, :].rearrange("(j p) a -> j (p a)", p=P)).then_inc(loaded, 16)

        @block.tensor
        def _(pe):
            pe.wait_ge(ptr_known, 1)
            pe.transpose(ps_row[0:NODE_TILES, 0:P], ptr, m.ident[:]).then_inc(turned, 1)
            pe.wait_ge(loaded, 16)
            pe.transpose(ps_next[:, 0:NODE_TILES], next_row[0:NODE_TILES, :],
                         m.ident[0:NODE_TILES, 0:NODE_TILES]).then_inc(turned, 1)

        @block.scalar
        def _(act):
            act.wait_ge(deg_known, 1)
            act.activation(s2, s0, ACT.Sqrt).then_inc(root, 1)

        @block.vector
        def _(dve):
            chain = Chain(dve, dve_step)
            chain(dve.memset(last[0:1, :], float(EPAD)))
            chain(dve.tensor_copy(rows, rows_i))
            chain(dve.tensor_tensor(rows, rows, over(m.node_no[:].unsqueeze(2), [P, NODE_TILES, P]), ALU.is_lt))
            chain(dve.tensor_reduce(in_tile, rows, AX.X, ALU.add))
            chain(dve.tensor_scalar(ptr, tiles_before, float(P), None, ALU.mult))
            chain(dve.tensor_tensor(ptr, ptr, in_tile, ALU.add))
            dve.engine_nop().then_inc(ptr_known, 1)
            dve.wait_ge(turned, 1)
            dve.tensor_copy(ptr_row[0:NODE_TILES, :], ps_row[0:NODE_TILES, 0:P]).then_inc(row_known, 1)
            dve.wait_ge(turned, 2)
            chain(dve.tensor_copy(ptr_next, ps_next[:, 0:NODE_TILES]))
            chain(dve.tensor_tensor(s0, ptr_next, ptr, ALU.subtract))
            chain(dve.tensor_scalar(m.has[:], s0, 1.0, None, ALU.min))
            chain(dve.tensor_scalar(s1, s0, 1.0, None, ALU.add))
            chain(dve.reciprocal(s0, s1))
            dve.engine_nop().then_inc(deg_known, 1)
            dve.wait_ge(root, 1)
            chain(dve.tensor_tensor(s0, s2, s2, ALU.mult))
            chain(dve.tensor_tensor(s0, s0, s1, ALU.mult))
            chain(dve.tensor_scalar(s0, s0, -0.5, 1.5, ALU.mult, ALU.add))
            chain(dve.tensor_tensor(m.dinv[:], s0, s2, ALU.mult))
            chain(dve.tensor_scalar(s0, m.node_no[:], m.node_no[:, 0:1], 2.0, ALU.subtract, ALU.mult))
            chain(dve.tensor_tensor(ptr, ptr, s0, ALU.add))
            chain(dve.tensor_scalar(s1, m.node_no[:], float(LANES * P), None, ALU.add))
            chain(dve.tensor_tensor(ptr, ptr, s1, ALU.subtract))
            chain(dve.tensor_tensor(ptr, ptr, m.has[:], ALU.mult))
            chain(dve.tensor_tensor(ptr, ptr, s1, ALU.add))
            chain(dve.tensor_copy(m.pos_first[:], ptr))


def store_table(nc, m, H, parts):
    ph, (stored,) = phase(nc, "table_stored")
    with ph, nc.Block(no_gpsimd_drain=True) as block:
        @block.sync
        def _(sp):
            for view, lo, hi in parts:
                sp.dma_start(m.d_table[H].rearrange("(j p) f -> p j f", p=P)[:, :, lo:hi], view).then_inc(stored, 16)
            sp.wait_ge(stored, 16 * len(parts))


def gather_half(pool, m, H, i, h, copied):
    at = i * (2 * U) + h * U
    pool.tensor_copy(m.idx[h][:], m.src[:, bass.ds(at, U)]).then_inc(copied, 1)
    pool.wait_ge(copied, 2 * i + h + 1)
    pool.nop(nofuse=True)
    W = F + H
    for k in range(U):
        yield pool.indirect_dma_start(m.ring[h][:, k * W:(k + 1) * W], None, m.d_table[H],
                                      bass.IndirectOffsetOnAxis(ap=m.idx[h][:, k:k + 1], axis=0))


def gather_rows(nc, m, H, a, weighted):
    W = F + H
    alpha = step_view(m, 1, H)
    raw, values = m.big[:, 8 * LANES:16 * LANES], step_view(m, 2, 8)
    tmp = step_view(m, 1, 8)
    ph, (copied, got0, got1, kept0, kept1, taken, scattered, spread_in, weights_in, dve_step) = phase(
        nc, "index_copied", "rows_in_0", "rows_in_1", "rows_out_0", "rows_out_1", "columns_taken",
        "nodes_scattered", "spread_loaded", "weights_loaded", "dve_step")
    group_turned, group_scored = ph.semaphore("group_turned"), ph.semaphore("group_scored")
    halves = [min((g + 1) * P, STEPS) // U for g in range(G)]
    assert P % U == 0
    got, out = (got0, got1), (kept0, kept1)
    carry = Carry(ph, m, 8)
    with ph, nc.Block() as block:

        @block.gpsimd
        def _(pool):
            for j in range(NODE_TILES):
                pool.indirect_dma_start(m.d_spread, bass.IndirectOffsetOnAxis(ap=m.pos_first[:, j:j + 1], axis=0),
                                        m.spread[:, j, :], None).then_inc(scattered, 16)
            if weighted:
                for g in range(G):
                    pool.indirect_dma_start(m.edge_w[:, g, :], None, a["edge_weight"],
                                            bass.IndirectOffsetOnAxis(ap=m.step_tile[:, g:g + 1], axis=0)).then_inc(weights_in, 16)

            def half(i, h, first):
                if not first:
                    pool.wait_ge(out[h], 16 * i)
                    pool.wait_ge(taken, 2 * i + h - 1)
                for dma in gather_half(pool, m, H, i, h, copied):
                    dma.then_inc(got[h], 16)

            half(0, 0, True)
            half(0, 1, True)
            with pool.Fori(1, PAIRS) as i:
                half(i, 0, False)
                half(i, 1, False)
            if weighted:
                pool.wait_ge(weights_in, 16 * G)

        @block.sync
        def _(sp):
            sp.wait_ge(scattered, 16 * NODE_TILES)
            sp.dma_start(raw.rearrange("p (g r) -> p g r", g=G),
                         m.d_spread[0:LANES * P, :].rearrange("(g p e) h -> p g (e h)", p=P, e=P)).then_inc(spread_in, 16)
            with sp.Fori(0, PAIRS) as i:
                for h in range(2):
                    sp.wait_ge(got[h], (i + 1) * (16 * U))
                    sp.dma_start(m.d_rows[H][:, bass.ds(i * (2 * U) + h * U, U), :].rearrange("e s f -> e (s f)"),
                                 m.ring[h][:, 0:U * W]).then_inc(out[h], 16)
            for h in range(2):
                sp.wait_ge(out[h], 16 * PAIRS)

        @block.scalar
        def _(act):
            with act.Fori(0, PAIRS) as i:
                for h in range(2):
                    act.wait_ge(got[h], (i + 1) * (16 * U))
                    rows = m.ring[h][:, 0:U * W].rearrange("p (u f) -> p u f", f=W)
                    act.copy(m.lane[:, bass.ds(i * (2 * U) + h * U, U), 0:H], rows[:, :, F:W]).then_inc(taken, 1)

        @block.tensor
        def _(pe):
            carry.tensor(pe, values, back=False)
            for g in range(G):
                pe.wait_ge(taken, halves[g])
                if g >= 2:
                    pe.wait_ge(group_scored, g - 1)
                for h in range(H):
                    t = pe.transpose(m.ps[g % 2][:, h * P:(h + 1) * P], m.lane[:, g * P:(g + 1) * P, h], m.ident[:])
                t.then_inc(group_turned, 1)

        @block.vector
        def _(dve):
            chain = Chain(dve, dve_step)
            dve.wait_ge(spread_in, 16)
            for h in range(8):
                data = raw.rearrange("p (l h) -> p h l", h=8)[:, h, :]
                chain(dve.tensor_tensor_scan(flat(values)[:, h, :], ge(m.keep[:]), data, 0.0, ALU.mult, ALU.add))
            before = carry.vector(dve, chain, m.open_row[:], 0.0, (ALU.mult, ALU.add), back=False)
            full = [P, 8, G, P]
            chain(dve.tensor_tensor(tmp, over(m.nostart[:].unsqueeze(1), full), before, ALU.mult))
            chain(dve.tensor_tensor(values, values, tmp, ALU.add))
            if weighted:
                dve.wait_ge(weights_in, 16 * G)
            for g in range(G):
                dve.wait_ge(group_turned, g + 1)
                one = alpha[:, :, g, :]
                chain(dve.tensor_tensor(one, m.ps[g % 2][:, 0:H * P].rearrange("p (h e) -> p h e", e=P),
                                        values[:, 0:H, g, :], ALU.add))
                dve.engine_nop().then_inc(group_scored, 1)
                if weighted:
                    chain(dve.tensor_tensor(one, one, over(m.edge_w[:, g:g + 1, :], [P, H, P]), ALU.mult))
                chain(leaky(dve, one))
                chain(dve.tensor_tensor(one, one, over(m.cap[:, g:g + 1, :], [P, H, P]), ALU.min))


def sum_edges(nc, m, H):
    R = F + H
    W = F + 8 if H else F
    C = F // H if H else F
    sums = (m.acc, m.acc_odd)
    D = U - ACT_HOTS if H else U
    names = ("index_copied", "rows_in_0", "rows_in_1", "act_difference_done", "act_onehot_done", "onehot_done",
             "messages_done", "product_done",
             "sum_done", "tails_done", "cleared", "joined")
    ph, (copied, got0, got1, difference, act_hot, hot_done, msg_done, prod, summed, tails, cleared, joined) = phase(nc, *names)
    got = (got0, got1)

    def at(i, h):
        return i * (2 * U) + h * U

    with ph, nc.Block() as block:
        def out(h, k):
            bank = h * BANKS + k // PER_BANK
            at = bank % 2 * 512 + (k % PER_BANK) * W
            return m.ps[bank // 2][:, at:at + W]

        if H == 0:
            @block.gpsimd
            def _(pool):
                def half(i, h, first):
                    if not first:
                        pool.wait_ge(prod, UNITS * (2 * i + h - 1))
                    for dma in gather_half(pool, m, 0, i, h, copied):
                        dma.then_inc(got[h], 16)

                half(0, 0, True)
                half(0, 1, True)
                with pool.Fori(1, PAIRS) as i:
                    half(i, 0, False)
                    half(i, 1, False)
        else:
            @block.sync
            def _(sp):
                def half(i, h, first):
                    if not first:
                        sp.wait_ge(msg_done, 2 * i + h - 1)
                    sp.dma_start(m.ring[h][:, 0:U * R], m.d_rows[H][:, bass.ds(at(i, h), U), :].rearrange("e s f -> e (s f)")
                                 ).then_inc(got[h], 16)

                half(0, 0, True)
                half(0, 1, True)
                with sp.Fori(1, PAIRS) as i:
                    half(i, 0, False)
                    half(i, 1, False)

            @block.gpsimd
            def _(pool):
                def half(i, h, first):
                    pool.wait_ge(got[h], (i + 1) * 16)
                    if not first:
                        pool.wait_ge(prod, UNITS * (2 * i + h - 1))
                    rows = m.ring[h][:, 0:U * R].rearrange("p (u f) -> p u f", f=R)[:, :, 0:F]
                    to = m.msg[h][:, 0:U * W].rearrange("p (u f) -> p u f", f=W)[:, :, 0:F]
                    coef = m.lane[:, bass.ds(at(i, h), U), 0:H]
                    pool.tensor_tensor(to.rearrange("p u (h c) -> p u h c", c=C), rows.rearrange("p u (h c) -> p u h c", c=C),
                                       over(coef.unsqueeze(3), [P, U, H, C]), ALU.mult).then_inc(msg_done, 1)

                half(0, 0, True)
                half(0, 1, True)
                with pool.Fori(1, PAIRS) as i:
                    half(i, 0, False)
                    half(i, 1, False)

            @block.scalar
            def _(act):
                def half(i, h, first):
                    if not first:
                        act.wait_ge(prod, UNITS * (2 * i + h - 1))
                    to = m.msg[h][:, 0:U * W].rearrange("p (u f) -> p u f", f=W)[:, :, F:W]
                    act.copy(to, m.lane[:, bass.ds(at(i, h), U), :]).then_inc(tails, 1)
                    for k in range(D, U):
                        act.activation(m.onehot[h][:, k, :], m.iota[:], ACT.Abs, bias=m.drel[:, bass.ds(at(i, h) + k, 1)],
                                       scale=-1.0).then_inc(difference, 1)
                    act.wait_ge(difference, ACT_HOTS * (2 * i + (h + 1)))
                    act.activation(m.onehot[h][:, D:U, :], m.onehot[h][:, D:U, :], ACT.Relu, bias=1.0, scale=-1.0).then_inc(act_hot, 1)

                half(0, 0, True)
                half(0, 1, True)
                with act.Fori(1, PAIRS) as i:
                    half(i, 0, False)
                    half(i, 1, False)

        @block.tensor
        def _(pe):
            def half(i, h, first):
                n = 2 * i + h
                pe.wait_ge(hot_done, n + 1)
                if H:
                    pe.wait_ge(msg_done, n + 1)
                    pe.wait_ge(tails, n + 1)
                    pe.wait_ge(act_hot, n + 1)
                else:
                    pe.wait_ge(got[h], (i + 1) * (16 * U))
                if not first:
                    pe.wait_ge(summed, UNITS * (n - 1))
                src = m.msg[h] if H else m.ring[h]
                for k in range(U):
                    mm = pe.matmul(out(h, k // 2), m.onehot[h][:, k, :], src[:, k * W:(k + 1) * W], start=(k % 2 == 0), stop=(k % 2 == 1))
                    if k % 2:
                        mm.then_inc(prod, 1)

            half(0, 0, True)
            half(0, 1, True)
            with pe.Fori(1, PAIRS) as i:
                half(i, 0, False)
                half(i, 1, False)

        @block.vector
        def _(dve):
            def onehot(i, h, first):
                if not first:
                    dve.wait_ge(prod, UNITS * (2 * i + h - 1))
                dve.tensor_tensor(m.onehot[h][:, 0:D, :], over(m.iota[:].unsqueeze(1), [P, D, P]),
                                  over(m.drel[:, bass.ds(at(i, h), D)].unsqueeze(2), [P, D, P]), ALU.is_equal).then_inc(hot_done, 1)

            def add_up(i, h):
                n = i * (2 * UNITS) + h * UNITS
                dve.load(m.j_regs, m.jrow[0:1, bass.ds(n, UNITS)])
                for k in range(UNITS):
                    j = dve.snap(m.j_regs[k], min_val=0, max_val=NODE_TILES - 1)
                    if k % PER_BANK == 0:
                        dve.wait_ge(prod, n + min(k + PER_BANK, UNITS))
                    if not (isinstance(n, int) and n + k < 2):
                        dve.wait_ge(summed, n + (k - 1))
                    to = sums[k % 2][:, bass.ds(j, 1), 0:W].rearrange("p a f -> p (a f)")
                    dve.tensor_tensor(to, to, out(h, k), ALU.add).then_inc(summed, 1)

            dve.memset(sums[0][:, :, 0:W], 0.0).then_inc(cleared, 1)
            dve.memset(sums[1][:, :, 0:W], 0.0).then_inc(cleared, 1)
            dve.wait_ge(cleared, 2)
            onehot(0, 0, True)
            onehot(0, 1, True)
            add_up(0, 0)
            with dve.Fori(1, PAIRS) as i:
                onehot(i, 0, False)
                add_up(i - 1, 1)
                onehot(i, 1, False)
                add_up(i, 0)
            add_up(PAIRS - 1, 1)
            dve.wait_ge(summed, STEPS // 2)
            dve.tensor_tensor(m.acc[:, :, 0:W], m.acc[:, :, 0:W], sums[1][:, :, 0:W], ALU.add).then_inc(joined, 1)
            dve.wait_ge(joined, 1)



def norm_rows(dve, chain, m, x, out, tmp, handoff):
    known, root = handoff
    mean, v, r, y = (t[:] for t in m.stat)
    full = [P, NODE_TILES, F]
    chain(dve.tensor_reduce(mean, x, AX.X, ALU.add))
    chain(dve.tensor_scalar(mean, mean, 1.0 / F, None, ALU.mult))
    chain(dve.tensor_tensor(out, x, over(mean.unsqueeze(2), full), ALU.subtract))
    chain(dve.tensor_tensor(tmp, out, out, ALU.mult))
    chain(dve.tensor_reduce(v, tmp, AX.X, ALU.add))
    chain(dve.tensor_scalar(v, v, 1.0 / F, 1e-5, ALU.mult, ALU.add))
    chain(dve.reciprocal(r, v))
    known()
    root()
    chain(dve.tensor_tensor(r, y, y, ALU.mult))
    chain(dve.tensor_tensor(r, r, v, ALU.mult))
    chain(dve.tensor_scalar(r, r, -0.5, 1.5, ALU.mult, ALU.add))
    chain(dve.tensor_tensor(r, r, y, ALU.mult))
    chain(dve.tensor_tensor(out, out, over(r.unsqueeze(2), full), ALU.mult))


class Handoff:

    def __init__(self, dve, known, done):
        self.dve, self.known_sem, self.done_sem, self.n = dve, known, done, 0

    def known(self):
        self.dve.engine_nop().then_inc(self.known_sem, 1)
        self.n += 1

    def root(self):
        self.dve.wait_ge(self.done_sem, self.n)

    def pair(self):
        return self.known, self.root


def act_turns(block, m, known, done, turns):
    @block.scalar
    def _(act):
        for n, turn in enumerate(turns):
            act.wait_ge(known, n + 1)
            turn(act).then_inc(done, 1)


def take_root(m):
    return lambda act: act.activation(m.stat[3][:], m.stat[2][:], ACT.Sqrt)


def take_exp(view):
    return lambda act: act.activation(view, view, ACT.Exp)


def row(m, name, shape):
    return over(m.weights[name][:].unsqueeze(1), shape)


def node_product(nc, m, src, dst, w_out, hidden=None):
    C = hidden[0].shape[1] // P if hidden else 0
    cols = BLK * P
    turned_sb = m.big[:, 0:cols]
    staged = m.big[:, cols:2 * cols]
    hid = [m.big[:, (2 + c) * cols:(3 + c) * cols] for c in range(C)]
    cuts = [(lo, min(lo + 512, cols)) for lo in range(0, cols, 512)]
    ph, (staged_up, turned, copied, hid_ready, hid_done, out_ready, out_copied) = phase(
        nc, "tiles_staged", "tiles_turned", "turned_copied", "hidden_ready", "hidden_done", "out_ready", "out_copied")
    ps_turn = m.ps[0]
    ps_h0 = m.ps[1]
    ps_h1 = m.ps[2]
    ps_out = m.ps[3]
    with ph, nc.Block(no_gpsimd_drain=True) as block:
        ps_h = (ps_h0, ps_h1)

        @block.gpsimd
        def _(pool):
            def tiles(i, first):
                if not first:
                    pool.wait_ge(turned, i)
                pool.tensor_copy(staged.rearrange("p (k f) -> p k f", f=F), src[:, bass.ds(i * BLK, BLK), :]).then_inc(staged_up, 1)

            tiles(0, True)
            with pool.Fori(1, NODE_TILES // BLK) as i:
                tiles(i, False)

        @block.tensor
        def _(pe):
            def tiles(i, first):
                pe.wait_ge(staged_up, i + 1)
                for k in range(BLK):
                    t = pe.transpose(ps_turn[:, k * P:(k + 1) * P], staged[:, k * P:(k + 1) * P], m.ident[:])
                t.then_inc(turned, 1)
                pe.wait_ge(copied, i + 1)
                for c in range(C):
                    if not (first and c < 2):
                        pe.wait_ge(hid_done, i * C + (c - 1))
                    for lo, hi in cuts:
                        t = pe.matmul(ps_h[c % 2][:, lo:hi], hidden[0][:, c * P:(c + 1) * P], turned_sb[:, lo:hi], start=True, stop=True)
                    t.then_inc(hid_ready, 1)
                if C:
                    pe.wait_ge(hid_done, (i + 1) * C)
                if not first:
                    pe.wait_ge(out_copied, i)
                for k in range(BLK):
                    for c in range(max(C, 1)):
                        lhs = hid[c] if C else turned_sb
                        rhs = w_out[:, c, :] if C else w_out[:]
                        t = pe.matmul(ps_out[:, k * P:(k + 1) * P], lhs[:, k * P:(k + 1) * P], rhs, start=(c == 0), stop=(c == max(C, 1) - 1))
                t.then_inc(out_ready, 1)

            tiles(0, True)
            with pe.Fori(1, NODE_TILES // BLK) as i:
                tiles(i, False)

        @block.scalar
        def _(act):
            def tiles(i, first):
                act.wait_ge(turned, i + 1)
                if not first:
                    act.wait_ge(out_ready, i)
                act.copy(turned_sb, ps_turn[:, 0:cols]).then_inc(copied, 1)
                for c in range(C):
                    act.wait_ge(hid_ready, i * C + (c + 1))
                    act.activation(hid[c], ps_h[c % 2][:, 0:cols], hidden[2], bias=hidden[1][:, c:c + 1]).then_inc(hid_done, 1)

            tiles(0, True)
            with act.Fori(1, NODE_TILES // BLK) as i:
                tiles(i, False)

        @block.vector
        def _(dve):
            with dve.Fori(0, NODE_TILES // BLK) as i:
                dve.wait_ge(out_ready, i + 1)
                dve.tensor_copy(dst[:, bass.ds(i * BLK, BLK), :], ps_out[:, 0:cols].rearrange("p (k f) -> p k f", f=F)).then_inc(out_copied, 1)


FULL = [P, NODE_TILES, F]


def dve_phase(nc, m, turns, body):
    ph, (step, known, done) = phase(nc, "dve_step", "act_input_known", "act_done")
    with ph, nc.Block(no_gpsimd_drain=True) as block:
        act_turns(block, m, known, done, turns)

        @block.vector
        def _(dve):
            body(dve, Chain(dve, step), Handoff(dve, known, done))


def gcn(nc, m, a):
    w = m.weights
    y, mid = m.node[0], m.node[1]
    dinv = over(m.dinv[:].unsqueeze(2), FULL)

    dve_phase(nc, m, [], lambda dve, chain, hand: chain(dve.tensor_tensor(y, m.x[:], dinv, ALU.mult)))
    store_table(nc, m, 0, [(y, 0, F)])
    sum_edges(nc, m, 0)

    def scaled(dve, chain, hand):
        chain(dve.tensor_tensor(mid, m.acc[:, :, 0:F], y, ALU.add))
        chain(dve.tensor_tensor(mid, mid, dinv, ALU.mult))

    dve_phase(nc, m, [], scaled)
    node_product(nc, m, mid, y, w["L0_W2T"], (w["L0_W1T"], w["L0_b1T"], ACT.Relu))
    dve_phase(nc, m, [], lambda dve, chain, hand: chain(dve.tensor_tensor(y, y, dinv, ALU.mult)))
    store_table(nc, m, 0, [(y, 0, F)])
    sum_edges(nc, m, 0)

    def finish(dve, chain, hand):
        scaled(dve, chain, hand)
        chain(dve.tensor_tensor(mid, mid, row(m, "L0_gnn_b2", FULL), ALU.add))
        chain(dve.tensor_scalar(mid, mid, 0.0, None, ALU.max))
        chain(dve.tensor_tensor(mid, mid, m.x[:], ALU.add))
        norm_rows(dve, chain, m, mid, m.x[:], y, hand.pair())

    dve_phase(nc, m, [take_root(m)], finish)


def heads(view, H):
    return view.rearrange("p j (h c) -> p j h c", h=H)


def node_scores(nc, m, H, att_src, att_dst, self_loops):
    tmp = m.node[1]

    def body(dve, chain, hand):
        xh = m.tab[:, :, 0:F]
        for name, out in ((att_src, m.a_src[:, :, 0:H]), (att_dst, m.spread[:, :, 0:H])):
            chain(dve.tensor_tensor(tmp, xh, row(m, name, FULL), ALU.mult))
            chain(dve.tensor_reduce(out, heads(tmp, H), AX.X, ALU.add))
        if self_loops:
            own = m.spread[:, :, H:2 * H]
            chain(dve.tensor_tensor(own, m.a_src[:, :, 0:H], m.spread[:, :, 0:H], ALU.add))
            chain(leaky(dve, own))

    dve_phase(nc, m, [], body)
    store_table(nc, m, H, [(m.tab[:, :, 0:F], 0, F), (m.a_src[:, :, 0:H], F, F + H)])


def step_view(m, i, H):
    return m.big[:, i * 8 * LANES:i * 8 * LANES + H * LANES].rearrange("p (h g e) -> p h g e", h=H, e=P)


def flat(view):
    return view.rearrange("p h g e -> p h (g e)")


def leaky(dve, view):
    return dve.scalar_tensor_tensor(out=view, in0=view, scalar=0.2, in1=view, op0=ALU.mult, op1=ALU.max)


class Carry:

    def __init__(self, ph, m, H):
        self.m, self.H = m, H
        self.last_known, self.rows_ready, self.scanned, self.back = (
            ph.semaphore(n) for n in ("last_lanes_known", "rows_ready", "rows_scanned", "carry_back"))
        self.ps_row, self.ps_back = m.ps[2], m.ps[3]

    def tensor(self, pe, local, back):
        m, H = self.m, self.H
        pe.wait_ge(self.last_known, 1)
        for g in range(G):
            t = pe.transpose(self.ps_row[0:H, g * P:(g + 1) * P], local[:, :, g, 0 if back else P - 1], m.ident[:])
        t.then_inc(self.rows_ready, 1)
        pe.wait_ge(self.scanned, 1)
        for g in range(G):
            lo = g * P + (1 if back else 0)
            t = pe.transpose(self.ps_back[:, g * 8:g * 8 + H], m.carry[0][0:H, lo:lo + P], m.ident[0:H, 0:H])
        t.then_inc(self.back, 1)

    def vector(self, dve, chain, open_row, initial, ops, back):
        m, H = self.m, self.H
        dve.engine_nop().then_inc(self.last_known, 1)
        chain(dve.memset(m.carry[0][0:H, LANES if back else 0:LANES + 1 if back else 1], initial))
        dve.wait_ge(self.rows_ready, 1)
        chain(dve.tensor_copy(m.carry[1][0:H, 0:LANES], self.ps_row[0:H, 0:LANES]))
        if back:
            out, last = m.carry[0][0:H, 0:LANES][:, ::-1], m.carry[1][0:H, 0:LANES][:, ::-1]
            open_row = open_row[:, ::-1]
        else:
            out, last = m.carry[0][0:H, 1:LANES + 1], m.carry[1][0:H, 0:LANES]
        chain(dve.tensor_tensor_scan(out, open_row, last, initial, *ops))
        dve.engine_nop().then_inc(self.scanned, 1)
        dve.wait_ge(self.back, 1)
        chain(dve.tensor_copy(m.step_carry[:, :, 0:H], self.ps_back[:, 0:8 * G].rearrange("p (g h) -> p g h", h=8)[:, :, 0:H]))
        return over(m.step_carry[:, :, 0:H].rearrange("p g h -> p h g").unsqueeze(3), [P, H, G, P])


def edge_coefficients(nc, m, H, self_loops):
    alpha, maxima, spread = step_view(m, 1, H), step_view(m, 0, H), step_view(m, 2, 8)
    tmp = step_view(m, 1, 8)[:, H:, :, :] if self_loops else step_view(m, 2, H)
    own = spread[:, H:, :, :] if self_loops else None
    full = [P, H, G, P]
    columns = 2 * H if self_loops else H
    ph, (dve_step, scores_known, exp_done, own_done, back_turned, back_copied) = phase(
        nc, "dve_step", "exponents_known", "exp_done", "own_done",
        "coefs_turned", "coefs_copied")
    forth, back = Carry(ph, m, H), Carry(ph, m, H)
    with ph, nc.Block(no_gpsimd_drain=True) as block:

        @block.tensor
        def _(pe):
            forth.tensor(pe, maxima, back=False)
            back.tensor(pe, maxima, back=True)
            pe.wait_ge(exp_done, 1)
            for c in range(columns):
                if c == H:
                    pe.wait_ge(own_done, 1)
                if c >= 2:
                    pe.wait_ge(back_copied, c - 1)
                coef = alpha[:, c] if c < H else own[:, c - H]
                for g in range(G):
                    t = pe.transpose(m.ps[c % 2][:, g * P:(g + 1) * P], coef[:, g, :], m.ident[:])
                t.then_inc(back_turned, 1)

        @block.scalar
        def _(act):
            act.wait_ge(scores_known, 1)
            act.activation(flat(alpha), flat(alpha), ACT.Exp).then_inc(exp_done, 1)
            if self_loops:
                act.wait_ge(scores_known, 2)
                act.activation(flat(own), flat(own), ACT.Exp).then_inc(exp_done, 1)
            for c in range(columns):
                act.wait_ge(back_turned, c + 1)
                act.copy(m.lane[:, :, c], m.ps[c % 2][:, 0:LANES]).then_inc(back_copied, 1)

        @block.vector
        def _(dve):
            chain = Chain(dve, dve_step)
            chain(dve.tensor_scalar(m.pen, ge(m.keep[:]), -1.0, -NEG, ALU.add, ALU.mult))
            chain(dve.tensor_scalar(m.open_pen[0:H, :], m.open_row[0:H, :], -1.0, -NEG, ALU.add, ALU.mult))
            for h in range(H):
                chain(dve.tensor_tensor_scan(flat(maxima)[:, h, :], m.pen, flat(alpha)[:, h, :], NEG, ALU.add, ALU.max))
            before = forth.vector(dve, chain, m.open_pen[0:H, :], NEG, (ALU.add, ALU.max), back=False)
            chain(dve.tensor_scalar(m.pen, ge(m.nostart[:]), -1.0, -NEG, ALU.add, ALU.mult))
            chain(dve.tensor_tensor(tmp, over(m.pen.rearrange("p (g e) -> p g e", e=P).unsqueeze(1), full), before, ALU.add))
            chain(dve.tensor_tensor(maxima, maxima, tmp, ALU.max))
            chain(dve.tensor_tensor(tmp, maxima, over(m.end[:].unsqueeze(1), full), ALU.mult))
            chain(dve.tensor_scalar(m.pen, ge(m.end[:]), -1.0, 1.0, ALU.mult, ALU.add))
            chain(dve.memset(m.pen.rearrange("p (g e) -> p g e", e=P)[:, :, P - 1:P], 0.0))
            for h in range(H):
                chain(dve.tensor_tensor_scan(flat(maxima)[:, h, ::-1], m.pen[:, ::-1], flat(tmp)[:, h, ::-1], 0.0,
                                             ALU.mult, ALU.add))
            before = back.vector(dve, chain, m.open_back[0:H, :], 0.0, (ALU.mult, ALU.add), back=True)
            chain(dve.tensor_tensor(tmp, over(m.noend[:].unsqueeze(1), full), before, ALU.mult))
            chain(dve.tensor_tensor(maxima, maxima, tmp, ALU.add))
            if self_loops:
                chain(dve.tensor_tensor(maxima, maxima, own, ALU.max))
            chain(dve.tensor_tensor(alpha, alpha, maxima, ALU.subtract))
            dve.engine_nop().then_inc(scores_known, 1)
            if self_loops:
                chain(dve.tensor_tensor(own, own, maxima, ALU.subtract))
                chain(dve.tensor_scalar(own, own, 0.0, None, ALU.min))
                dve.engine_nop().then_inc(scores_known, 1)
                dve.wait_ge(exp_done, 2)
                chain(dve.tensor_tensor(own, own, over(m.end[:].unsqueeze(1), full), ALU.mult))
                dve.engine_nop().then_inc(own_done, 1)


def attention(nc, m, H, att_src, att_dst, self_loops, a):
    node_scores(nc, m, H, att_src, att_dst, self_loops)
    gather_rows(nc, m, H, a, not self_loops)
    edge_coefficients(nc, m, H, self_loops)
    sum_edges(nc, m, H)


def finish_sums(dve, chain, m, H, out, self_loops, eps):
    den = m.acc[:, :, F:F + H]
    c = F // H
    wide = [P, NODE_TILES, H, c]
    src = m.acc[:, :, 0:F]
    if self_loops:
        own = m.self_p[:, :, 0:H]
        chain(dve.tensor_scalar(m.stat[0][:], m.has[:], -1.0, 1.0, ALU.mult, ALU.add))
        chain(dve.tensor_tensor(own, m.acc[:, :, F + H:F + 2 * H], over(m.stat[0][:].unsqueeze(2), [P, NODE_TILES, H]), ALU.add))
        chain(dve.tensor_tensor(heads(out, H), heads(m.tab[:, :, 0:F], H), over(own.unsqueeze(3), wide), ALU.mult))
        chain(dve.tensor_tensor(out, out, src, ALU.add))
        chain(dve.tensor_tensor(den, den, own, ALU.add))
        src = out
    if eps:
        chain(dve.tensor_scalar(den, den, eps, None, ALU.add))
    inv = m.inv[:, :, 0:H]
    chain(dve.reciprocal(inv, den))
    chain(dve.tensor_tensor(heads(out, H), heads(src, H), over(inv.unsqueeze(3), wide), ALU.mult))


def gat(nc, m, a):
    w = m.weights
    node_product(nc, m, m.x, m.tab[:, :, 0:F], w["L1_gnn_W"])
    attention(nc, m, 4, "L1_gnn_att_src", "L1_gnn_att_dst", True, a)
    o, t, u = m.node

    def finish(dve, chain, hand):
        finish_sums(dve, chain, m, 4, o, True, 1e-16)
        chain(dve.tensor_tensor(o, o, row(m, "L1_gnn_bias", FULL), ALU.add))
        norm_rows(dve, chain, m, o, t, u, hand.pair())
        chain(dve.tensor_tensor(t, t, row(m, "L1_gnn_ln_w", FULL), ALU.mult))
        chain(dve.tensor_tensor(t, t, row(m, "L1_gnn_ln_b", FULL), ALU.add))
        chain(dve.tensor_scalar(u, t, 0.0, w["L1_gnn_prelu_w"][:, 0:1], ALU.min, ALU.mult))
        chain(dve.tensor_scalar(t, t, 0.0, None, ALU.max))
        chain(dve.tensor_tensor(t, t, u, ALU.add))
        chain(dve.tensor_tensor(t, t, m.x[:], ALU.add))
        norm_rows(dve, chain, m, t, m.x[:], u, hand.pair())

    dve_phase(nc, m, [take_root(m)] * 2, finish)


def weighted_gat(nc, m, a):
    w = m.weights
    node_product(nc, m, m.x, m.tab[:, :, 0:F], w["L2_gnn_W"])
    attention(nc, m, 8, "L2_gnn_att_l", "L2_gnn_att_r", False, a)
    o, t, u = m.node
    node_product(nc, m, m.x, u, w["L2_gnn_W_res"])

    def finish(dve, chain, hand):
        finish_sums(dve, chain, m, 8, o, False, 1e-16)
        chain(dve.tensor_scalar(t, o, 0.0, None, ALU.min))
        hand.known()
        chain(dve.tensor_scalar(o, o, 0.0, -1.0, ALU.max, ALU.add))
        hand.root()
        chain(dve.tensor_tensor(o, o, t, ALU.add))
        chain(dve.tensor_tensor(o, o, u, ALU.add))
        chain(dve.tensor_tensor(o, o, m.x[:], ALU.add))
        norm_rows(dve, chain, m, o, m.x[:], t, hand.pair())

    dve_phase(nc, m, [take_exp(t), take_root(m)], finish)


def transformer_gat(nc, m, a):
    w = m.weights
    o, t, u = m.node

    def before(dve, chain, hand):
        norm_rows(dve, chain, m, m.x[:], t, u, hand.pair())
        chain(dve.tensor_tensor(t, t, row(m, "L3_gnn_ln1_g", FULL), ALU.mult))
        chain(dve.tensor_tensor(t, t, row(m, "L3_gnn_ln1_b", FULL), ALU.add))

    dve_phase(nc, m, [take_root(m)], before)
    node_product(nc, m, t, m.tab[:, :, 0:F], w["L3_gnn_W"])
    attention(nc, m, 4, "L3_gnn_att_src", "L3_gnn_att_dst", True, a)

    def middle(dve, chain, hand):
        finish_sums(dve, chain, m, 4, o, True, 0.0)
        chain(dve.tensor_tensor(o, o, row(m, "L3_gnn_gat_b", FULL), ALU.add))
        chain(dve.tensor_tensor(o, o, m.x[:], ALU.add))
        norm_rows(dve, chain, m, o, t, u, hand.pair())
        chain(dve.tensor_tensor(t, t, row(m, "L3_gnn_ln2_g", FULL), ALU.mult))
        chain(dve.tensor_tensor(t, t, row(m, "L3_gnn_ln2_b", FULL), ALU.add))

    dve_phase(nc, m, [take_root(m)], middle)
    node_product(nc, m, t, u, w["L3_gnn_w2"], (w["L3_gnn_w1"], w["L3_b1T"], ACT.Gelu))

    def finish(dve, chain, hand):
        chain(dve.tensor_tensor(u, u, row(m, "L3_gnn_b2", FULL), ALU.add))
        chain(dve.tensor_tensor(u, u, o, ALU.add))
        chain(dve.tensor_tensor(u, u, m.x[:], ALU.add))
        norm_rows(dve, chain, m, u, m.x[:], t, hand.pair())

    dve_phase(nc, m, [take_root(m)], finish)


def store_output(nc, m, out):
    full = N // P
    ph, (stored,) = phase(nc, "output_stored")
    with ph, nc.Block() as block:
        @block.sync
        def _(sp):
            sp.dma_start(out[0:full * P, :].rearrange("(j p) f -> p j f", p=P), m.x[:, 0:full, :]).then_inc(stored, 16)
            sp.dma_start(out[full * P:N, :], m.x[0:N - full * P, full, :]).then_inc(stored, 16)
            sp.wait_ge(stored, 32)


def program(nc, a, out):
    Phase.used, Phase.count = [], 0
    with ExitStack() as ctx:
        m = Net()
        allocate(nc, ctx, m)
        load_parameters(nc, m, a)
        step_tables(nc, m, a)
        step_edges(nc, m, a)
        row_pointers(nc, m, a)
        end_of_layer(nc)
        for n, layer in enumerate((gcn, gat, weighted_gat, transformer_gat)):
            with ExitStack() as layer_ctx:
                load_weights(nc, layer_ctx, m, a, n)
                layer(nc, m, a)
                end_of_layer(nc)
        store_output(nc, m, out)


def layout(inputs):
    import numpy as np
    v = {k: np.asarray(x) for k, x in inputs.items()}
    a = {"x": np.zeros((NPAD, F), np.float32)}
    a["x"][:N] = v["x"]

    def edges(x, fill):
        padded = np.full(EPAD, fill, x.dtype)
        padded[:E] = x
        return padded

    dst = edges(v["dst"], NPAD - 1)
    a["dst"] = dst.reshape(EDGE_TILES, P)
    a["dst_before"] = np.concatenate([np.full(1, -1, dst.dtype), dst[:-1]]).reshape(EDGE_TILES, P)
    a["dst_after"] = np.concatenate([dst[1:], np.full(1, -1, dst.dtype)]).reshape(EDGE_TILES, P)
    a["tile_last"] = np.ascontiguousarray(a["dst"][:, -1]).reshape(1, EDGE_TILES)
    a["src"] = edges(v["src"], 0).reshape(EDGE_TILES, P)
    a["edge_weight"] = edges(v["edge_weight"], 0).reshape(EDGE_TILES, P)
    for n in ("L0_gnn_b2", "L1_gnn_att_src", "L1_gnn_att_dst", "L1_gnn_bias", "L1_gnn_ln_w", "L1_gnn_ln_b",
              "L1_gnn_prelu_w", "L2_gnn_att_l", "L2_gnn_att_r", "L3_gnn_ln1_g", "L3_gnn_ln1_b", "L3_gnn_att_src",
              "L3_gnn_att_dst", "L3_gnn_gat_b", "L3_gnn_ln2_g", "L3_gnn_ln2_b", "L3_gnn_b2"):
        a[n] = v[n].reshape(1, -1)
    for n in ("L1_gnn_W", "L2_gnn_W", "L2_gnn_W_res", "L3_gnn_W", "L3_gnn_w1", "L3_gnn_w2"):
        a[n] = v[n]
    a["L0_W1T"] = v["L0_gnn_W1"].T
    a["L0_W2T"] = v["L0_gnn_W2"].T
    a["L0_b1T"] = v["L0_gnn_b1"].reshape(-1, P).T
    a["L3_b1T"] = v["L3_gnn_b1"].reshape(-1, P).T
    return {k: np.ascontiguousarray(x) for k, x in a.items()}


def kernel(**inputs):
    import concourse.bacc as bacc
    from concourse.bass_utils import run_bass_kernel_spmd

    nc = bacc.Bacc("TRN2", target_bir_lowering=False, num_devices=1)
    arrays = {"in_" + k: x for k, x in layout(inputs).items()}
    a = {k[3:]: nc.dram_tensor(k, x.shape, mybir.dt.from_np(x.dtype), kind="ExternalInput").ap() for k, x in arrays.items()}
    out = nc.dram_tensor("out", (N, F), F32, kind="ExternalOutput").ap()
    program(nc, a, out)
    return run_bass_kernel_spmd(nc, [arrays], core_ids=[0]).results[0]["out"]
```
